# Optimizing a Trainium2 kernel written in Bass

```python
import numpy as np
import jax
import jax.numpy as jnp

def _softmax(x, axis=-1):
    return jax.nn.softmax(x, axis=axis)

def _gelu(x):
    return jax.nn.gelu(x, approximate=True)

def _silu(x):
    return jax.nn.silu(x)

def _sigmoid(x):
    return jax.nn.sigmoid(x)

def _layernorm(x, axis=-1, eps=1e-05):
    m = jnp.mean(x, axis=axis, keepdims=True)
    v = jnp.var(x, axis=axis, keepdims=True)
    return (x - m) / jnp.sqrt(v + eps)

def _scatter_add(tgt, idx, src, axis=0):
    return tgt.at[idx].add(src)

def _segment_sum(src, seg, n):
    return jax.ops.segment_sum(src, seg, n)
kernel_name = 'mk_adj_resnorm_d4_adj_r2_0249e4'

def setup_inputs(seed: int=0):
    np.random.seed(seed)
    _w = jnp.asarray

    def _rec_inputs():
        import jax
        import jax.numpy as jnp
        _gk = jax.random.key(seed)
        x = 7.22e-05 + 1 * jax.random.normal(jax.random.fold_in(_gk, 1), (8, 1024, 128), jnp.float32)
        _w = (1.0 + jnp.arange(1024, dtype=jnp.float32)) ** (-0.5)
        _w = _w / _w.mean()
        _pij = jnp.clip(0.00390625 * _w[:, None] * _w[None, :], 0.0, 1.0)
        _a = jax.random.uniform(jax.random.fold_in(_gk, 2), (1024, 1024)) < _pij
        _a = jnp.logical_or(_a, jnp.eye(1024, dtype=bool))
        _af = _a.astype(jnp.float32)
        _af = _af * jax.random.uniform(jax.random.fold_in(_gk, 3), (1024, 1024), jnp.float32, 0.05, 1)
        adj = _af
        return (x, adj)
    x, adj = _rec_inputs()

    def _L0_gnn_setup():
        import jax, jax.numpy as jnp
        import numpy as np
        B, N, F_IN, F_OUT = (8, 4096, 128, 128)
        EPS = 1e-12
        key = jax.random.key(seed)
        k1, k2, k3, k4 = jax.random.split(key, 4)
        x = jax.random.normal(k1, (B, N, F_IN), dtype=jnp.float32)
        adj = jax.random.uniform(k2, (N, N), dtype=jnp.float32)
        weight = jax.random.normal(k3, (F_IN, F_OUT), dtype=jnp.float32) * 0.05
        bias = jax.random.normal(k4, (F_OUT,), dtype=jnp.float32) * 0.05
        return {'x': x, 'adj': adj, 'weight': weight, 'bias': bias}
    _L0_gnn_all = _L0_gnn_setup()
    _L0_gnn_in = {k: v for k, v in _L0_gnn_all.items() if k in ('weight', 'bias')}
    del _L0_gnn_all

    def _L1_gnn_setup():
        import jax, jax.numpy as jnp
        import numpy as np
        B, N, D = (4, 4096, 128)
        key = jax.random.key(seed)
        kx, ka, kq, kk, kv = jax.random.split(key, 5)
        x = jax.random.normal(kx, (B, N, D), dtype=jnp.float32)
        mask = (jax.random.uniform(ka, (N, N)) < 0.05).astype(jnp.float32)
        A_shape = jnp.clip(mask + jnp.eye(N, dtype=jnp.float32), 0.0, 1.0)
        q = jax.random.normal(kq, (D, D), dtype=jnp.float32)
        k = jax.random.normal(kk, (D, D), dtype=jnp.float32)
        v = jax.random.normal(kv, (D, D), dtype=jnp.float32)
        return {'x': x, 'A_shape': A_shape, 'q': q, 'k': k, 'v': v}
    _L1_gnn_all = _L1_gnn_setup()
    _L1_gnn_in = {k: v for k, v in _L1_gnn_all.items() if k in ('q', 'k', 'v')}
    del _L1_gnn_all

    def _L2_gnn_setup():
        import jax, jax.numpy as jnp
        import numpy as np
        B, N, D, OUT = (8, 1024, 128, 128)
        key = jax.random.key(seed)
        k1, k2, k3, k4, k5, k6 = jax.random.split(key, 6)
        stdv = 1.0 / np.sqrt(OUT)
        inputs = jax.random.normal(k1, (B, N, D), dtype=jnp.float32)
        relation = jax.random.normal(k2, (N, N), dtype=jnp.float32)
        gl = 1.0 / np.sqrt(2 * D + 1)
        g_w = jax.random.uniform(k3, (2 * D + 1,), minval=-gl, maxval=gl, dtype=jnp.float32)
        g_b = jax.random.uniform(k4, (), minval=-gl, maxval=gl, dtype=jnp.float32)
        weight = jax.random.uniform(k5, (D, OUT), minval=-stdv, maxval=stdv, dtype=jnp.float32)
        bias = jax.random.uniform(k6, (OUT,), minval=-stdv, maxval=stdv, dtype=jnp.float32)
        return {'inputs': inputs, 'relation': relation, 'g_w': g_w, 'g_b': g_b, 'weight': weight, 'bias': bias}
    _L2_gnn_all = _L2_gnn_setup()
    _L2_gnn_in = {k: v for k, v in _L2_gnn_all.items() if k in ('g_w', 'g_b', 'weight', 'bias')}
    del _L2_gnn_all

    def _L3_gnn_setup():
        import jax, jax.numpy as jnp
        import numpy as np
        B, N, CIN, COUT, K = (8192, 17, 128, 128, 3)

        def _cheb_basis(adj):
            n = adj.shape[0]
            d_inv_sqrt = jnp.sum(adj, axis=-1) ** (-0.5)
            eye = jnp.eye(n, dtype=adj.dtype)
            L = eye - d_inv_sqrt[:, None] * adj * d_inv_sqrt[None, :]
            T2 = 2.0 * (L @ L) - eye
            return jnp.stack([eye, L, T2])
        key = jax.random.key(seed)
        kx, ka, kw = jax.random.split(key, 3)
        x = jax.random.normal(kx, (B, N, CIN), dtype=jnp.float32)
        adj = jax.random.uniform(ka, (N, N), dtype=jnp.float32)
        weight = jax.random.normal(kw, (K, 1, CIN, COUT), dtype=jnp.float32) * 0.05
        bias = jnp.zeros((1, 1, COUT), dtype=jnp.float32)
        return {'x': x, 'adj': adj, 'weight': weight, 'bias': bias}
    _L3_gnn_all = _L3_gnn_setup()
    _L3_gnn_in = {k: v for k, v in _L3_gnn_all.items() if k in ('weight', 'bias')}
    del _L3_gnn_all
    return {'x': x, 'adj': adj, 'L0_gnn_weight': _L0_gnn_in['weight'], 'L0_gnn_bias': _L0_gnn_in['bias'], 'L1_gnn_q': _L1_gnn_in['q'], 'L1_gnn_k': _L1_gnn_in['k'], 'L1_gnn_v': _L1_gnn_in['v'], 'L2_gnn_g_w': _L2_gnn_in['g_w'], 'L2_gnn_g_b': _L2_gnn_in['g_b'], 'L2_gnn_weight': _L2_gnn_in['weight'], 'L2_gnn_bias': _L2_gnn_in['bias'], 'L3_gnn_weight': _L3_gnn_in['weight'], 'L3_gnn_bias': _L3_gnn_in['bias']}

def reference(x, adj, L0_gnn_weight, L0_gnn_bias, L1_gnn_q, L1_gnn_k, L1_gnn_v, L2_gnn_g_w, L2_gnn_g_b, L2_gnn_weight, L2_gnn_bias, L3_gnn_weight, L3_gnn_bias):
    import jax
    import jax.numpy as jnp

    def _L0_gnn_ref(x, adj, weight, bias):
        import jax, jax.numpy as jnp
        import numpy as np
        B, N, F_IN, F_OUT = (8, 4096, 128, 128)
        EPS = 1e-12
        y = jnp.einsum('nm,bmf->bnf', adj, x)
        y = y + x
        y = jnp.einsum('bnf,fo->bno', y, weight) + bias
        norm = jnp.sqrt(jnp.sum(y * y, axis=2, keepdims=True))
        y = y / jnp.maximum(norm, EPS)
        return y

    def _L1_gnn_ref(x, A_shape, q, k, v):
        import jax, jax.numpy as jnp
        import numpy as np
        B, N, D = (4, 4096, 128)
        input_dimension = x.shape[-1]
        Q = x @ q
        K = x @ k
        A = jnp.einsum('bnd,bmd->bnm', Q, K)
        A = A / jnp.sqrt(jnp.float32(input_dimension))
        A = jnp.tanh(A / 8.0) * 8.0
        A = jnp.exp(A) * A_shape
        A = A / jnp.sum(A, axis=-1, keepdims=True)
        out = A @ x @ v
        return out

    def _L2_gnn_ref(inputs, relation, g_w, g_b, weight, bias):
        import jax, jax.numpy as jnp
        import numpy as np
        B, N, D, OUT = (8, 1024, 128, 128)
        b, n, d = inputs.shape
        w_j = g_w[:d]
        w_i = g_w[d:2 * d]
        w_r = g_w[2 * d]
        sj = inputs @ w_j
        si = inputs @ w_i
        res = si[:, :, None] + sj[:, None, :] + relation[None] * w_r + g_b
        agg = jnp.einsum('bij,bjd->bid', res, inputs)
        return agg @ weight + bias

    def _L3_gnn_ref(x, adj, weight, bias):
        import jax, jax.numpy as jnp
        import numpy as np
        B, N, CIN, COUT, K = (8192, 17, 128, 128, 3)

        def _cheb_basis(adj):
            n = adj.shape[0]
            d_inv_sqrt = jnp.sum(adj, axis=-1) ** (-0.5)
            eye = jnp.eye(n, dtype=adj.dtype)
            L = eye - d_inv_sqrt[:, None] * adj * d_inv_sqrt[None, :]
            T2 = 2.0 * (L @ L) - eye
            return jnp.stack([eye, L, T2])
        mul_L = _cheb_basis(adj)
        h = jnp.einsum('knm,bmc->kbnc', mul_L, x)
        h = jnp.einsum('kbnc,kcd->kbnd', h, weight[:, 0])
        out = jnp.sum(h, axis=0) + bias
        return jax.nn.relu(out)
    x = _layernorm(x + _L0_gnn_ref(x, adj, L0_gnn_weight, L0_gnn_bias), axis=-1)
    x = _layernorm(x + _L1_gnn_ref(x, adj, L1_gnn_q, L1_gnn_k, L1_gnn_v), axis=-1)
    x = _layernorm(x + _L2_gnn_ref(x, adj, L2_gnn_g_w, L2_gnn_g_b, L2_gnn_weight, L2_gnn_bias), axis=-1)
    x = _layernorm(x + _L3_gnn_ref(x, adj, L3_gnn_weight, L3_gnn_bias), axis=-1)
    return x

_drawn_inputs = setup_inputs


def setup_inputs(seed=0):
    import zlib

    import numpy as np

    out = dict(_drawn_inputs(seed))
    spreads = {'L3_gnn_bias': (0.0, 0.1)}
    factors = {'L2_gnn_bias': 28.066}
    for name, (base, spread) in spreads.items():
        noise = np.random.default_rng([zlib.crc32(name.encode()), seed]).standard_normal(out[name].shape)
        drawn = base * np.exp(spread * noise) if base else spread * noise
        out[name] = jnp.asarray(drawn.astype(out[name].dtype))
    for name, factor in factors.items():
        out[name] = (out[name] * factor).astype(out[name].dtype)
    return out
```

```python
import concourse.bass as bass
from concourse import mybir
from contextlib import ExitStack
import numpy as np

F32 = mybir.dt.float32
F16 = mybir.dt.float16
U32 = mybir.dt.uint32
ALU = mybir.AluOpType
ACT = mybir.ActivationFunctionType
AX = mybir.AxisListType

B, N, D = 8, 1024, 128
P = 128
C = N // P
HALF = 512
EPS = 1e-5
NORM_FLOOR = 1e-12
MIN_MAX = 1e-30
POW2_MASK = 0x7F800000

X_UP = 16.0
SUM_UP = 4096.0
W_DOWN = 1.0 / 32
Q_DOWN = 1.0 / 4
ADJ_UP = 256.0
LAP_UP = 64.0
LO_UP = 2048.0
P_UP = 16.0
Y0_DOWN = 1.0 / 1024
Y2_DOWN = 1.0 / 1024
TANH_CAP = 8.0
AVW = 130
RING = 3
LN_LINKS = 6


class Count:

    def __init__(self, eng, sem, b, per):
        self.eng, self.sem, self.base, self.per, self.n = eng, sem, b * per, per, 0

    def mark(self, ins):
        ins.then_inc(self.sem, 1)
        self.n += 1

    def wait(self):
        self.eng.wait_ge(self.sem, self.base + self.n)

    def link(self, ins):
        self.mark(ins)
        self.wait()

    def end(self):
        assert self.n == self.per, (self.n, self.per)


def adj_resnorm(nc, x, adj, w0, b0, q, k, v, gw, gb, w2, b2, w3, b3, out):
    ctx = ExitStack()
    with ctx:
        def sb(name, shape, dt=F32):
            return ctx.enter_context(nc.sbuf_tensor(name, shape, dt))

        def ps(name, shape):
            return ctx.enter_context(nc.psum_tensor(name, shape, F32))

        def sem(name):
            return ctx.enter_context(nc.semaphore(name))

        adjT = sb("adjT", [P, C, N])
        a_hi = sb("a_hi", [P, C, N], F16)
        a_lo = sb("a_lo", [P, C, N], F16)
        lap = sb("lap", [P, 2, C, N], F16)
        adj_rows = lap[:].rearrange("p a c n -> p (a c n)").bitcast(F32).rearrange("p (c n) -> p c n", c=C)
        ident = sb("ident", [P, P])
        ident_up = sb("ident_up", [P, P], F16)
        ones = sb("ones", [P, P])
        w0_sb, q_sb, k_sb, v_sb, w2_sb = (sb(n_, [P, D]) for n_ in ("w0_sb", "q_sb", "k_sb", "v_sb", "w2_sb"))
        w3_sb = sb("w3_sb", [P, 3, D])
        qT, kT, m_sb = sb("qT", [P, D]), sb("kT", [P, D]), sb("m_sb", [P, D])
        w3c = sb("w3c", [P, 3, D])
        w0s, ms, vs, w2s = (sb(n_, [P, 2, D], F16) for n_ in ("w0s", "ms", "vs", "w2s"))
        w3s = sb("w3s", [P, 3, 2, D], F16)
        b0_bc, b2_bc, b3_bc, wj_bc, wi_bc = (sb(n_, [P, D]) for n_ in ("b0_bc", "b2_bc", "b3_bc", "wj_bc", "wi_bc"))
        wr_gb = sb("wr_gb", [P, 2])
        wmax, wpow, winv = (sb(n_, [P, 5]) for n_ in ("wmax", "wpow", "winv"))
        coef = sb("coef", [P, 8])
        c_w0, c_tanh, c_v, c_l2, c_u, c_o = (coef[:, j:j + 1] for j in range(6))
        deg, dis = sb("deg", [P, C]), sb("dis", [P, C])
        x0 = sb("x0", [P, C, D])
        xmax, xpow, xinv, c_y0 = (sb(n_, [P, 1]) for n_ in ("xmax", "xpow", "xinv", "c_y0"))
        x0s = sb("x0s", [P, 2, C, D], F16)
        yT = sb("yT", [P, 2, N], F16)
        x1 = sb("x1", [P, C, D])
        x1T = sb("x1T", [P, 2, N], F16)
        gr = sb("gr", [P, 2, N], F16)
        vhi = sb("vhi", [P, C, AVW], F16)
        vlo = sb("vlo", [P, C, D], F16)
        vhs = sb("vhs", [P, C, AVW], F16)
        att = sb("att", [P, RING, N])
        p_hi, p_lo = sb("p_hi", [P, RING, N], F16), sb("p_lo", [P, RING, N], F16)
        x2 = sb("x2", [P, C, D])
        x2s = sb("x2s", [P, 2, C, D], F16)
        one_sj = sb("one_sj", [P, C, 2])
        sig = sb("sig", [P, C])
        tmp = sb("tmp", [P, C, D])
        xb = sb("xb", [P, 2, P])
        r2b = sb("r2b", [P, D])
        x3 = sb("x3", [P, C, D])
        xq = sb("xq", [P, 2, N], F16)
        pq = sb("pq", [P, C, D])
        u = sb("u", [P, C, D])
        outb = sb("outb", [P, C, D])
        stats = sb("stats", [P, C, 2, 3])
        pair = sb("pair", [P, C, 2])
        minus_half = sb("minus_half", [P, C])
        small = sb("small", [P, 8, C])
        rsum, rinv = sb("rsum", [P, 9]), sb("rinv", [P, C])
        dis_bc = pq[:].rearrange("p c d -> p (c d)")
        lap_f = u[:].rearrange("p c d -> p (c d)")
        lap_g = outb[:].rearrange("p c d -> p (c d)")

        r0 = ps("r0", [P, N])
        r1 = ps("r1", [P, N])
        av = ps("av", [P, 3, HALF])
        m7 = ps("m7", [P, HALF])
        r2 = av[:].rearrange("p a n -> p (a n)")[:, 0:N]

        def cd(ap):
            return ap.rearrange("p (c d) -> p c d", c=C)

        names = ("w_in wq_in x_in ident_ok const_ok qk_t qk_c m_mm w_max w_sum w_red "
                 "tr adj_hi adj_cp adj_lo deg_ok diag_ok dbc_mm lap_st lap_hi lap_lo "
                 "ln0_r ln1_r ln2_r ln3_r norm_r dis_ok x_max x_sum x_st x_hi x_lo "
                 "y0_mm y0_hi y0_lo p0_mm e0_c e0 ln0 x1_ok x1t_mm x1t_hi x1t_lo g_mm g_hi g_lo v_mm v_hi v_s v_lo "
                 "s_mm th ex pm ph pl av_mm e1a e1a_c ln1 x2_ok x2_hi sj_c e1b "
                 "xx_mm xb_ok y2_mm y2_hi y2_lo rr_mm p2_mm l2_c ln2 x3_ok x3t_mm x3t_hi x3t_lo "
                 "r_mm r_hi r_lo p_mm p_cp u_mm u_ok t_mm q_ok q_hi q_lo o_mm fa f_c ln3 fin stored").split()
        S = {n_: sem(n_) for n_ in names}
        adj_in = [sem(f"adj_in{c}") for c in range(C)]

        block = ctx.enter_context(nc.Block())

        def iterations(eng, body):
            body(-1, True, False, False, False)
            body(0, True, True, False, False)
            body(1, True, True, True, False)
            body(2, True, True, True, True)
            with eng.Fori(3, B - 1) as i:
                body(i, True, True, True, True)
            body(B - 1, False, True, True, True)
            body(B, False, False, True, True)
            body(B + 1, False, False, False, True)

        @block.sync
        def _(sp):
            adj_v = adj.rearrange("(c p) m -> c p m", p=P)
            for c in range(C):
                sp.dma_start(adj_rows[:, c, :], adj_v[c]).then_inc(adj_in[c], 16)
            x_v = x.rearrange("b (c p) d -> b p c d", p=P)
            out_v = out.rearrange("b (c p) d -> b p c d", p=P)

            def body(i, nxt, cur, prev, last):
                if nxt and cur:
                    sp.wait_ge(S["e0"], i + 1)
                    sp.dma_start(x0[:], x_v[i + 1]).then_inc(S["x_in"], 16)
                if last:
                    sp.wait_ge(S["fin"], i - 1)
                    sp.dma_start(out_v[i - 2], outb[:]).then_inc(S["stored"], 16)

            iterations(sp, body)
            sp.wait_ge(S["stored"], 16 * B)

        @block.gpsimd
        def _(pool):
            nc.gpsimd.memset(ident[:], 0.0).then_inc(S["ident_ok"], 1)
            pool.wait_ge(S["ident_ok"], 1)
            nc.gpsimd.affine_select(out=ident[:], in_=ident[:], compare_op=ALU.not_equal, fill=1.0, base=0,
                                    pattern=[[-1, P]], channel_multiplier=1).then_inc(S["ident_ok"], 1)

            nc.gpsimd.memset(minus_half[:], -0.5).then_inc(S["ident_ok"], 1)
            pool.wait_ge(S["ident_ok"], 3)

            def inverse_root(dst, src):
                return nc.gpsimd.tensor_tensor(dst, src, minus_half[:], ALU.pow)

            def norm_root(name, b):
                pool.wait_ge(S[name], LN_LINKS * b + 5)
                inverse_root(small[:, 5], small[:, 6]).then_inc(S[name + "_r"], 1)

            def body(i, nxt, cur, prev, last):
                if last:
                    norm_root("ln3", i - 2)
                if isinstance(i, int) and i == -1:
                    pool.wait_ge(S["deg_ok"], C)
                    inverse_root(dis[:], deg[:]).then_inc(S["dis_ok"], 1)
                if prev:
                    norm_root("ln2", i - 1)
                if nxt:
                    pool.wait_ge(S["e0_c"], 6 * (i + 2))
                    inverse_root(small[:, 5], small[:, 6]).then_inc(S["norm_r"], 1)
                    norm_root("ln0", i + 1)
                if cur:
                    norm_root("ln1", i)

            iterations(pool, body)

        @block.scalar
        def _(act):
            x_v = x.rearrange("b (c p) d -> b p c d", p=P)
            act.dma_start(x0[:], x_v[0]).then_inc(S["x_in"], 16)
            for dst, src in ((q_sb, q), (k_sb, k)):
                act.dma_start(dst[:], src).then_inc(S["wq_in"], 16)
            for dst, src in ((w0_sb, w0), (v_sb, v), (w2_sb, w2)):
                act.dma_start(dst[:], src).then_inc(S["w_in"], 16)
            act.dma_start(w3_sb[:], w3.rearrange("k o c d -> c (k o) d")).then_inc(S["w_in"], 16)
            for dst, src in ((b0_bc[:], b0), (b2_bc[:], b2), (b3_bc[:], b3.rearrange("a b d -> (a b d)")),
                             (wj_bc[:], gw[0:D]), (wi_bc[:], gw[D:2 * D]), (wr_gb[:, 0:1], gw[2 * D:2 * D + 1]),
                             (wr_gb[:, 1:2], gb)):
                act.dma_start(dst, src.partition_broadcast(P)).then_inc(S["w_in"], 16)

            for c in range(C):
                buf = (r0, r1)[c % 2]
                act.wait_ge(S["tr"], c + 1)
                src = cd(buf[:])
                nc.scalar.activation(a_hi[:, :, c * P:(c + 1) * P], src, ACT.Copy, scale=ADJ_UP).then_inc(S["adj_hi"], 1)
                nc.scalar.activation(adjT[:, :, c * P:(c + 1) * P], src, ACT.Copy,
                                     scale=LO_UP * P_UP).then_inc(S["adj_cp"], 1)

            def split_hi(dst, src, scale, done):
                nc.scalar.activation(dst, src, ACT.Copy, scale=scale).then_inc(S[done], 1)

            def lap_hi_part(first, last_):
                for c in range(first, last_):
                    act.wait_ge(S["lap_st"], 2 * (c + 1))
                    nc.scalar.activation(lap[:, 0, c, :], (lap_f, lap_g)[c % 2], ACT.Copy).then_inc(S["lap_hi"], 1)

            def body(i, nxt, cur, prev, last):
                t8 = i * C

                def y2_half(h):
                    act.wait_ge(S["y2_mm"], 2 * (i - 1) + h + 1)
                    if h == 0:
                        act.wait_ge(S["p0_mm"], i + 1 if nxt or cur else B)
                    split_hi(yT[:, 0, h * HALF:(h + 1) * HALF], m7[:], Y2_DOWN, "y2_hi")

                def x0_hi():
                    act.wait_ge(S["x_st"], 5 * (i + 2))
                    if cur:
                        act.wait_ge(S["y0_mm"], i + 1)
                    nc.scalar.activation(x0s[:, 0], x0[:], ACT.Copy, scale=xinv[:]).then_inc(S["x_hi"], 1)

                def p_hi_part(t):
                    act.wait_ge(S["pm"], t8 + t + 1)
                    if cur and not (isinstance(i, int) and i == 0 and t < RING):
                        act.wait_ge(S["av_mm"], t8 + t - RING + 1)
                    s = slot(t)
                    nc.scalar.activation(p_hi[:, s], att[:, s], ACT.Copy, scale=1.0 / LO_UP).then_inc(S["ph"], 1)

                if cur:
                    for t in range(C):
                        s = slot(t)
                        act.wait_ge(S["s_mm"], t8 + t + 1)
                        if not (isinstance(i, int) and i == 0 and t < RING):
                            act.wait_ge(S["pl"], t8 + t - RING + 1)
                        nc.scalar.activation(att[:, s], (r1, r0)[t % 2][:], ACT.Tanh, scale=c_tanh).then_inc(S["th"], 1)
                        act.wait_ge(S["th"], t8 + t + 1)
                        nc.scalar.activation(att[:, s], att[:, s], ACT.Exp, scale=TANH_CAP).then_inc(S["ex"], 1)
                        if t >= 1:
                            p_hi_part(t - 1)
                        if t == 5 and prev:
                            y2_half(0)
                        if t == 6 and nxt:
                            x0_hi()
                    p_hi_part(C - 1)
                else:
                    if prev:
                        y2_half(0)
                    if nxt:
                        x0_hi()
                if prev:
                    y2_half(1)
                    act.wait_ge(S["x3t_mm"], i)
                    if last:
                        act.wait_ge(S["o_mm"], i - 1)
                    split_hi(xq[:, 0], r0[:], X_UP, "x3t_hi")
                if isinstance(i, int) and i in (-1, 0):
                    lap_hi_part(*((0, C // 2), (C // 2, C))[i + 1])
                if nxt:
                    act.wait_ge(S["y0_mm"], i + 2)
                    if prev:
                        act.wait_ge(S["p2_mm"], i)
                    split_hi(yT[:, 0], r1[:], Y0_DOWN, "y0_hi")
                if prev:
                    act.wait_ge(S["r_mm"], i)
                    split_hi(gr[:, 0], r2, W_DOWN, "r_hi")
                    act.wait_ge(S["p_mm"], i)
                    if last:
                        act.wait_ge(S["q_lo"], i - 1)
                    split_hi(pq[:], cd(r0[:]), W_DOWN * Q_DOWN, "p_cp")
                if nxt:
                    act.wait_ge(S["x1t_mm"], i + 2)
                    split_hi(x1T[:, 0], r1[:], X_UP, "x1t_hi")
                if prev:
                    act.wait_ge(S["q_ok"], i)
                    act.wait_ge(S["u_mm"], i)
                    nc.scalar.activation(xq[:, 0], pq[:].rearrange("p c d -> p (c d)"), ACT.Copy).then_inc(S["q_hi"], 1)
                if nxt:
                    act.wait_ge(S["g_mm"], i + 2)
                    if prev:
                        act.wait_ge(S["t_mm"], i)
                    split_hi(gr[:, 0], r2, W_DOWN, "g_hi")
                    act.wait_ge(S["v_mm"], i + 2)
                    if cur:
                        act.wait_ge(S["av_mm"], C * (i + 1))
                    split_hi(vhi[:, :, 0:D], cd(r1[:]), W_DOWN, "v_hi")
                    act.wait_ge(S["v_hi"], i + 2)
                    nc.scalar.activation(vhs[:, :, 0:D], vhi[:, :, 0:D], ACT.Copy, scale=1.0 / LO_UP).then_inc(S["v_s"], 1)
                if cur:
                    act.wait_ge(S["x2_ok"], i + 1)
                    if prev:
                        act.wait_ge(S["y2_mm"], 2 * i)
                    nc.scalar.activation(x2s[:, 0], x2[:], ACT.Copy, scale=X_UP).then_inc(S["x2_hi"], 1)

            def slot(t):
                return t % RING

            iterations(act, body)

        @block.vector
        def _(dve):
            tt = nc.vector.tensor_tensor
            ts = nc.vector.tensor_scalar
            stt = nc.vector.scalar_tensor_tensor

            def row(ap):
                return ap.unsqueeze(1).to_broadcast([P, C, D])

            def col(ap):
                return ap.unsqueeze(2).to_broadcast([P, C, D])

            def layer_norm(sem_name, b, src, dst):
                ch = Count(dve, S[sem_name], b, LN_LINKS)
                for j in range(C):
                    last_ = nc.vector.bn_stats(stats[:, j].rearrange("p a k -> p (a k)"), src[:, j])
                ch.link(last_)
                me, mo = stats[:, :, 0, 1], stats[:, :, 1, 1]
                tt(small[:, 0], me, mo, ALU.add)
                tt(small[:, 1], me, mo, ALU.subtract)
                ch.link(tt(small[:, 2], stats[:, :, 0, 2], stats[:, :, 1, 2], ALU.add))
                tt(small[:, 3], small[:, 1], small[:, 1], ALU.mult)
                ch.link(ts(small[:, 4], small[:, 0], -0.5, None, ALU.mult))
                ch.link(stt(small[:, 5], small[:, 3], D / 4.0, small[:, 2], ALU.mult, ALU.add))
                ch.link(ts(small[:, 6], small[:, 5], 1.0 / D, EPS, ALU.mult, ALU.add))
                dve.wait_ge(S[sem_name + "_r"], b + 1)
                ch.link(tt(small[:, 7], small[:, 4], small[:, 5], ALU.mult))
                ch.end()
                for j in range(C):
                    last_ = ts(dst[:, j], src[:, j], small[:, 5, j:j + 1], small[:, 7, j:j + 1], ALU.mult, ALU.add)
                return last_

            nc.vector.memset(ones[:], 1.0)
            nc.vector.memset(one_sj[:, :, 0:1], 1.0)
            nc.vector.memset(vhi[:, :, D:D + 1], 1.0)
            nc.vector.memset(vhs[:, :, D:D + 1], 1.0 / LO_UP).then_inc(S["const_ok"], 1)

            def x0_max(b):
                dve.wait_ge(S["x_in"], 16 * (b + 1))
                nc.vector.tensor_reduce(xmax[:], x0[:].rearrange("p c d -> p (c d)"), AX.X, ALU.max,
                                        apply_absolute_value=True).then_inc(S["x_max"], 1)

            def x0_scales(b):
                ch = Count(dve, S["x_st"], b, 5)
                dve.wait_ge(S["x_sum"], b + 1)
                ch.link(ts(xpow[:], m7[:, 4:5], MIN_MAX, None, ALU.max))
                ch.link(ts(xpow[:].bitcast(U32), xpow[:].bitcast(U32), POW2_MASK, None, ALU.bitwise_and))
                ch.link(nc.vector.reciprocal(xinv[:], xpow[:]))
                ch.link(ts(xinv[:], xinv[:], SUM_UP, None, ALU.mult))
                ch.mark(ts(c_y0[:], xpow[:], c_w0, None, ALU.mult))
                ch.end()

            def x0_lo(b):
                dve.wait_ge(S["x_hi"], b + 1)
                stt(x0s[:, 1], x0[:], xinv[:], x0s[:, 0], ALU.mult, ALU.subtract).then_inc(S["x_lo"], 1)

            x0_max(0)
            dve.wait_ge(S["qk_t"], 1)
            nc.vector.tensor_copy(qT[:], m7[:, 0:P])
            nc.vector.tensor_copy(kT[:], m7[:, P:2 * P]).then_inc(S["qk_c"], 1)
            dve.wait_ge(S["w_in"], 16 * 11)
            tt(w3c[:, 2], w3_sb[:, 0], w3_sb[:, 2], ALU.subtract)
            nc.vector.tensor_copy(w3c[:, 0], w3_sb[:, 2])
            nc.vector.tensor_copy(w3c[:, 1], w3_sb[:, 1])
            dve.wait_ge(S["m_mm"], 1)
            nc.vector.tensor_copy(m_sb[:], m7[:, 2 * P:3 * P]).then_inc(S["w_max"], 1)
            dve.wait_ge(S["w_max"], 1)
            for j, w in enumerate((w0_sb[:], m_sb[:], v_sb[:], w2_sb[:], w3c[:].rearrange("p k d -> p (k d)"))):
                nc.vector.tensor_reduce(wmax[:, j:j + 1], w, AX.X, ALU.max,
                                        apply_absolute_value=True).then_inc(S["w_max"], 1)
            dve.wait_ge(S["w_sum"], 1)
            ch = Count(dve, S["w_red"], 0, 12)
            ch.link(ts(wpow[:], m7[:, 3 * P:3 * P + 5], MIN_MAX, None, ALU.max))
            ch.link(ts(wpow[:].bitcast(U32), wpow[:].bitcast(U32), POW2_MASK, None, ALU.bitwise_and))
            ch.link(nc.vector.reciprocal(winv[:], wpow[:]))
            ch.link(ts(winv[:], winv[:], SUM_UP, None, ALU.mult))
            parts = ((w0_sb[:], w0s[:, 0], w0s[:, 1]), (m_sb[:], ms[:, 0], ms[:, 1]), (v_sb[:], vs[:, 0], vs[:, 1]),
                     (w2_sb[:], w2s[:, 0], w2s[:, 1]), (w3c[:], w3s[:, :, 0], w3s[:, :, 1]))
            for j, (w, hi, lo) in enumerate(parts):
                ch.link(ts(hi, w, winv[:, j:j + 1], None, ALU.mult))
                stt(lo, w, winv[:, j:j + 1], hi, ALU.mult, ALU.subtract)
            xw = X_UP * SUM_UP
            ts(c_w0, wpow[:, 0:1], 1.0 / (SUM_UP * ADJ_UP * Y0_DOWN * SUM_UP), None, ALU.mult)
            ts(c_tanh, wpow[:, 1:2], 1.0 / (X_UP * xw * W_DOWN * float(np.sqrt(float(D))) * TANH_CAP), None, ALU.mult)
            ts(c_v, wpow[:, 2:3], 1.0 / (xw * W_DOWN), None, ALU.mult)
            ts(c_u, wpow[:, 4:5], 1.0 / xw, None, ALU.mult)
            ts(c_o, wpow[:, 4:5], 1.0 / (xw * W_DOWN * Q_DOWN * LAP_UP), None, ALU.mult)
            ch.link(ts(c_l2, wpow[:, 3:4], 1.0 / (xw * ADJ_UP * Y2_DOWN), None, ALU.mult))
            ch.link(ts(c_l2, c_l2, wr_gb[:, 0:1], None, ALU.mult))
            dve.wait_ge(S["ident_ok"], 2)
            ch.link(ts(ident_up[:], ident[:], ADJ_UP, None, ALU.mult))
            ch.end()

            for c in range(C):
                dve.wait_ge(adj_in[c], 16)
                nc.vector.tensor_reduce(deg[:, c:c + 1], adj_rows[:, c, :], AX.X, ALU.add).then_inc(S["deg_ok"], 1)
                dve.wait_ge(S["adj_cp"], c + 1)
                sl = slice(c * P, (c + 1) * P)
                stt(a_lo[:, :, sl], adjT[:, :, sl], ADJ_UP / (LO_UP * P_UP), a_hi[:, :, sl],
                    ALU.mult, ALU.subtract).then_inc(S["adj_lo"], 1)

            def laplacian(first, last_):
                if first == 0:
                    dve.wait_ge(S["dis_ok"], 1)
                    for c in range(C):
                        diag = tmp[:, c]
                        l_ = ts(diag, ident[:], dis[:, c:c + 1], None, ALU.mult)
                    l_.then_inc(S["diag_ok"], 1)
                    dve.wait_ge(S["dbc_mm"], 1)
                    ts(dis_bc, r0[:], -LAP_UP / (LO_UP * P_UP), None, ALU.mult).then_inc(S["diag_ok"], 1)
                    dve.wait_ge(S["diag_ok"], 2)
                for c in range(first, last_):
                    f = (lap_f, lap_g)[c % 2]
                    if c >= 2:
                        dve.wait_ge(S["lap_hi"], c - 1)
                    stt(f, adjT[:, c, :], dis[:, c:c + 1], dis_bc, ALU.mult, ALU.mult).then_inc(S["lap_st"], 1)
                    dve.wait_ge(S["lap_st"], 2 * c + 1)
                    blk = f[:, c * P:(c + 1) * P]
                    stt(blk, ident[:], LAP_UP, blk, ALU.mult, ALU.add).then_inc(S["lap_st"], 1)
                    dve.wait_ge(S["lap_hi"], c + 1)
                    tt(lap[:, 1, c, :], f, lap[:, 0, c, :], ALU.subtract).then_inc(S["lap_lo"], 1)

            def body(i, nxt, cur, prev, last):
                t8 = i * C

                def split_lo(dst, src, scale, hi, hi_sem, hi_count, done):
                    dve.wait_ge(S[hi_sem], hi_count)
                    stt(dst, src, scale, hi, ALU.mult, ALU.subtract).then_inc(S[done], 1)

                def mask(t):
                    dve.wait_ge(S["ex"], t8 + t + 1)
                    s = t % RING
                    tt(att[:, s], att[:, s], adjT[:, t, :], ALU.mult).then_inc(S["pm"], 1)

                def p_lo_part(t):
                    dve.wait_ge(S["ph"], t8 + t + 1)
                    s = t % RING
                    stt(p_lo[:, s], p_hi[:, s], -LO_UP, att[:, s], ALU.mult, ALU.add).then_inc(S["pl"], 1)

                def y2_half(h):
                    sl = slice(h * HALF, (h + 1) * HALF)
                    split_lo(yT[:, 1, sl], m7[:], Y2_DOWN, yT[:, 0, sl], "y2_hi", 2 * (i - 1) + h + 1, "y2_lo")

                def finish():
                    ch = Count(dve, S["f_c"], i - 2, 1)
                    if not (isinstance(i, int) and i == 2):
                        dve.wait_ge(S["stored"], 16 * (i - 2))
                    dve.wait_ge(S["fa"], i - 1)
                    ch.link(stt(outb[:], u[:], 0.0, x3[:], ALU.max, ALU.add))
                    ch.end()
                    layer_norm("ln3", i - 2, outb, outb).then_inc(S["fin"], 1)

                if last:
                    dve.wait_ge(S["o_mm"], i - 1)
                    stt(u[:], cd(r0[:]), c_o, u[:], ALU.mult, ALU.add).then_inc(S["fa"], 1)
                if nxt:
                    if cur:
                        x0_max(i + 1)
                    if prev:
                        dve.wait_ge(S["xx_mm"], i)
                    x0_scales(i + 1)
                if prev:
                    dve.wait_ge(S["xx_mm"], i)
                    nc.vector.tensor_copy(xb[:], m7[:, 0:2].unsqueeze(2).to_broadcast([P, 2, P])).then_inc(S["xb_ok"], 1)
                if cur:
                    for t in range(C):
                        mask(t)
                        if t >= 1:
                            p_lo_part(t - 1)
                        if t == 1 and last:
                            finish()
                        if t == 5 and prev:
                            y2_half(0)
                        if t == 7 and nxt:
                            x0_lo(i + 1)
                    p_lo_part(C - 1)
                else:
                    if last:
                        finish()
                    if prev:
                        y2_half(0)
                    if nxt:
                        x0_lo(i + 1)
                if prev:
                    y2_half(1)
                    ch = Count(dve, S["l2_c"], i - 1, 3)
                    dve.wait_ge(S["rr_mm"], i)
                    tt(r2b[:], m7[:, P:2 * P], b2_bc[:], ALU.add)
                    for j in range(C):
                        l_ = stt(x3[:, j], m7[:, 0:P], sig[:, j:j + 1], x2[:, j], ALU.mult, ALU.add)
                    ch.link(l_)
                    ch.link(tt(x3[:], x3[:], row(r2b[:]), ALU.add))
                    dve.wait_ge(S["p2_mm"], i)
                    ch.link(stt(x3[:], cd(r0[:]), c_l2, x3[:], ALU.mult, ALU.add))
                    ch.end()
                    layer_norm("ln2", i - 1, x3, x3).then_inc(S["x3_ok"], 1)
                if cur:
                    ch = Count(dve, S["e1a_c"], i, 2)
                    dve.wait_ge(S["av_mm"], C * (i + 1))
                    for k_ in range(3):
                        w = min(3, C - 3 * k_)
                        l_ = nc.vector.reciprocal(rsum[:, 3 * k_:3 * k_ + w], av[:, k_, D:D + AVW * (w - 1) + 1:AVW])
                    ch.link(l_)
                    ch.link(ts(rinv[:], rsum[:, 0:C], c_v, None, ALU.mult))
                    ch.end()
                    for j in range(C):
                        o = (j % 3) * AVW
                        l_ = stt(x2[:, j], av[:, j // 3, o:o + D], rinv[:, j:j + 1], x1[:, j], ALU.mult, ALU.add)
                    l_.then_inc(S["e1a"], 1)
                if isinstance(i, int) and i in (-1, 0):
                    laplacian(*((0, C // 2), (C // 2, C))[i + 1])
                if prev:
                    split_lo(xq[:, 1], r0[:], X_UP, xq[:, 0], "x3t_hi", i, "x3t_lo")
                if nxt:
                    split_lo(yT[:, 1], r1[:], Y0_DOWN, yT[:, 0], "y0_hi", i + 2, "y0_lo")
                if prev:
                    split_lo(gr[:, 1], r2, W_DOWN, gr[:, 0], "r_hi", i, "r_lo")
                if nxt:
                    ch = Count(dve, S["e0_c"], i + 1, 6)
                    dve.wait_ge(S["p0_mm"], i + 2)
                    ch.link(stt(x1[:], cd(r1[:]), c_y0[:], row(b0_bc[:]), ALU.mult, ALU.add))
                    for j in range(C):
                        l_ = nc.vector.bn_stats(stats[:, j].rearrange("p a k -> p (a k)"), x1[:, j])
                    ch.link(l_)
                    ch.link(tt(pair[:], stats[:, :, :, 1], stats[:, :, :, 1], ALU.mult))
                    ch.link(stt(pair[:], pair[:], D / 2.0, stats[:, :, :, 2], ALU.mult, ALU.add))
                    ch.link(tt(small[:, 0], pair[:, :, 0], pair[:, :, 1], ALU.add))
                    ch.link(ts(small[:, 6], small[:, 0], NORM_FLOOR * NORM_FLOOR, None, ALU.max))
                    dve.wait_ge(S["norm_r"], i + 2)
                    for j in range(C):
                        l_ = stt(x1[:, j], x1[:, j], small[:, 5, j:j + 1], x0[:, j], ALU.mult, ALU.add)
                    l_.then_inc(S["e0"], 1)
                    dve.wait_ge(S["e0"], i + 2)
                    ch.end()
                    layer_norm("ln0", i + 1, x1, x1).then_inc(S["x1_ok"], 1)
                if prev:
                    dve.wait_ge(S["u_mm"], i)
                    stt(u[:], cd(r2), c_u, row(b3_bc[:]), ALU.mult, ALU.add).then_inc(S["u_ok"], 1)
                if nxt:
                    split_lo(x1T[:, 1], r1[:], X_UP, x1T[:, 0], "x1t_hi", i + 2, "x1t_lo")
                if prev:
                    dve.wait_ge(S["t_mm"], i)
                    dve.wait_ge(S["p_cp"], i)
                    stt(pq[:], cd(r0[:]), 2.0 * Q_DOWN / LAP_UP, pq[:], ALU.mult, ALU.add).then_inc(S["q_ok"], 1)
                    dve.wait_ge(S["q_hi"], i)
                    tt(xq[:, 1], pq[:].rearrange("p c d -> p (c d)"), xq[:, 0], ALU.subtract).then_inc(S["q_lo"], 1)
                if nxt:
                    split_lo(gr[:, 1], r2, W_DOWN, gr[:, 0], "g_hi", i + 2, "g_lo")
                    dve.wait_ge(S["v_s"], i + 2)
                    split_lo(vlo[:], cd(r1[:]), W_DOWN, vhi[:, :, 0:D], "v_hi", i + 2, "v_lo")
                if cur:
                    dve.wait_ge(S["e1a"], i + 1)
                    layer_norm("ln1", i, x2, x2).then_inc(S["x2_ok"], 1)
                    dve.wait_ge(S["x2_ok"], i + 1)
                    ch = Count(dve, S["sj_c"], i, 4)
                    ch.link(tt(tmp[:], x2[:], row(wj_bc[:]), ALU.mult))
                    ch.link(nc.vector.tensor_reduce(one_sj[:, :, 1], tmp[:], AX.X, ALU.add))
                    ch.link(tt(tmp[:], x2[:], row(wi_bc[:]), ALU.mult))
                    ch.link(nc.vector.tensor_reduce(sig[:], tmp[:], AX.X, ALU.add))
                    ch.end()
                    ts(sig[:], sig[:], wr_gb[:, 1:2], None, ALU.add)
                    dve.wait_ge(S["x2_hi"], i + 1)
                    stt(x2s[:, 1], x2[:], X_UP, x2s[:, 0], ALU.mult, ALU.subtract).then_inc(S["e1b"], 1)

            iterations(dve, body)

        @block.tensor
        def _(pe):
            mm = nc.tensor.matmul

            pe.wait_ge(S["ident_ok"], 2)
            pe.wait_ge(S["wq_in"], 32)
            nc.tensor.transpose(m7[:, 0:P], q_sb[:], ident[:])
            nc.tensor.transpose(m7[:, P:2 * P], k_sb[:], ident[:]).then_inc(S["qk_t"], 1)
            pe.wait_ge(S["qk_c"], 1)
            mm(m7[:, 2 * P:3 * P], qT[:], kT[:], start=True, stop=True).then_inc(S["m_mm"], 1)
            pe.wait_ge(S["const_ok"], 1)
            pe.wait_ge(S["w_max"], 6)
            mm(m7[:, 3 * P:3 * P + 5], ones[:], wmax[:], start=True, stop=True).then_inc(S["w_sum"], 1)
            for c in range(C):
                pe.wait_ge(adj_in[c], 16)
                if c >= 2:
                    pe.wait_ge(S["adj_cp"], c - 1)
                buf = (r0, r1)[c % 2]
                for m in range(C):
                    l_ = nc.tensor.transpose(buf[:, m * P:(m + 1) * P], adj_rows[:, c, m * P:(m + 1) * P], ident[:])
                l_.then_inc(S["tr"], 1)

            def split_product(dst, s_hi, s_lo, m_hi, m_lo, start, stop):
                mm(dst, s_hi, m_hi, start=start, stop=False, skip_group_check=True)
                mm(dst, s_hi, m_lo, start=False, stop=False, skip_group_check=True)
                return mm(dst, s_lo, m_hi, start=False, stop=stop, skip_group_check=True)

            def transpose_nodes(dst, src):
                for j in range(C):
                    l_ = nc.tensor.transpose(dst[:, j * P:(j + 1) * P], src[:, j], ident[:])
                return l_

            def project(dst, srcT, w_hi, w_lo):
                for j in range(C):
                    sl = slice(j * P, (j + 1) * P)
                    l_ = split_product(dst[:, sl], srcT[:, 0, sl], srcT[:, 1, sl], w_hi, w_lo, True, True)
                return l_

            def apply_laplacian(dst, src, first, last_):
                for j in range(first, last_):
                    sl = slice(j * P, (j + 1) * P)
                    for m in range(C):
                        ms_ = slice(m * D, (m + 1) * D)
                        l_ = split_product(dst[:, sl], lap[:, 0, m, sl], lap[:, 1, m, sl], src[:, 0, ms_], src[:, 1, ms_],
                                           m == 0, m == C - 1)
                return l_

            def body(i, nxt, cur, prev, last):
                t8 = i * C

                def scores(t):
                    if t == 0:
                        pe.wait_ge(S["v_lo"], i + 1)
                    elif t == 1:
                        if last:
                            pe.wait_ge(S["fa"], i - 1)
                    else:
                        pe.wait_ge(S["th"], t8 + t - 1)
                    ts_ = slice(t * P, (t + 1) * P)
                    dst = (r1, r0)[t % 2]
                    for h in range(2):
                        hs = slice(h * HALF, (h + 1) * HALF)
                        l_ = split_product(dst[:, hs], x1T[:, 0, ts_], x1T[:, 1, ts_], gr[:, 0, hs], gr[:, 1, hs], True, True)
                    l_.then_inc(S["s_mm"], 1)

                def attend(t):
                    pe.wait_ge(S["pl"], t8 + t + 1)
                    if t == 0 and not (isinstance(i, int) and i == 0):
                        pe.wait_ge(S["e1a"], i)
                    s = t % RING
                    for j in range(C):
                        o, sl = (j % 3) * AVW, slice(j * P, (j + 1) * P)
                        acc = av[:, j // 3, o:o + D + 1]
                        mm(acc, p_hi[:, s, sl], vhi[:, t, 0:D + 1], start=(t == 0 and j % 3 == 0), stop=False,
                           skip_group_check=True)
                        mm(acc[:, 0:D], p_hi[:, s, sl], vlo[:, t, :], start=False, stop=False, skip_group_check=True)
                        l_ = mm(acc, p_lo[:, s, sl], vhs[:, t, 0:D + 1], start=False, stop=(t == C - 1),
                                skip_group_check=True)
                    l_.then_inc(S["av_mm"], 1)

                def adj_x2(part):
                    h, m0 = part // 4, 2 * (part % 4)
                    hs = slice(h * HALF, (h + 1) * HALF)
                    if part == 0:
                        pe.wait_ge(S["e1b"], i)
                        pe.wait_ge(S["xb_ok"], i)
                    if part == 4:
                        pe.wait_ge(S["y2_lo"], 2 * i - 1)
                    for m in range(m0, m0 + 2):
                        l_ = split_product(m7[:], x2s[:, 0, m], x2s[:, 1, m], a_hi[:, m, hs], a_lo[:, m, hs],
                                           m == 0, m == C - 1)
                    if part % 4 == 3:
                        l_.then_inc(S["y2_mm"], 1)

                def sums():
                    pe.wait_ge(S["e1b"], i)
                    if last:
                        pe.wait_ge(S["x3_ok"], i - 1)
                    for j in range(C):
                        l_ = mm(m7[:, 0:2], x2[:, j], one_sj[:, j], start=(j == 0), stop=(j == C - 1))
                    l_.then_inc(S["xx_mm"], 1)

                def adj_x0(first, last_):
                    for m in range(first, last_):
                        if m == 0:
                            pe.wait_ge(S["x_lo"], i + 2)
                        for h in range(2):
                            hs = slice(h * HALF, (h + 1) * HALF)
                            split_product(r1[:, hs], x0s[:, 0, m], x0s[:, 1, m], a_hi[:, m, hs], a_lo[:, m, hs],
                                          m == 0, False)
                        blk = r1[:, m * P:(m + 1) * P]
                        mm(blk, x0s[:, 0, m], ident_up[:], start=False, stop=False, skip_group_check=True)
                        l_ = mm(blk, x0s[:, 1, m], ident_up[:], start=False, stop=(m == C - 1), skip_group_check=True)
                    if last_ == C:
                        l_.then_inc(S["y0_mm"], 1)

                if cur:
                    scores(0)
                    scores(1)
                if nxt:
                    if last:
                        pe.wait_ge(S["x3_ok"], i - 1)
                    if isinstance(i, int) and i == -1:
                        pe.wait_ge(S["w_red"], 1)
                    pe.wait_ge(S["x_max"], i + 2)
                    mm(m7[:, 4:5], ones[:], xmax[:], start=True, stop=True).then_inc(S["x_sum"], 1)
                if prev:
                    sums()
                for t in range(2, C):
                    if cur:
                        scores(t)
                        attend(t - 2)
                    if prev:
                        adj_x2(t - 2)
                if cur:
                    attend(C - 2)
                if prev:
                    adj_x2(C - 2)
                    adj_x2(C - 1)
                if cur:
                    attend(C - 1)
                if prev:
                    pe.wait_ge(S["y2_lo"], 2 * i)
                    mm(m7[:, 0:P], xb[:, 0], w2_sb[:], start=True, stop=True)
                    mm(m7[:, P:2 * P], xb[:, 1], w2_sb[:], start=True, stop=True).then_inc(S["rr_mm"], 1)
                    if cur:
                        pe.wait_ge(S["th"], t8 + C)
                    elif last:
                        pe.wait_ge(S["fa"], i - 1)
                    project(r0, yT, w2s[:, 0], w2s[:, 1]).then_inc(S["p2_mm"], 1)
                if isinstance(i, int) and i == -1:
                    pe.wait_ge(S["adj_lo"], C)
                    pe.wait_ge(S["w_red"], 12)
                if nxt:
                    if cur:
                        pe.wait_ge(S["th"], t8 + C - 1)
                    adj_x0(0, 1)
                if isinstance(i, int) and i == -1:
                    pe.wait_ge(S["diag_ok"], 1)
                    for c in range(C):
                        l_ = mm(r0[:, c * P:(c + 1) * P], ones[:], tmp[:, c], start=True, stop=True)
                    l_.then_inc(S["dbc_mm"], 1)
                if nxt:
                    adj_x0(1, C - 1)
                if prev:
                    pe.wait_ge(S["x3_ok"], i)
                    transpose_nodes(r0, x3).then_inc(S["x3t_mm"], 1)
                if nxt:
                    adj_x0(C - 1, C)
                if prev:
                    pe.wait_ge(S["x3t_lo"], i)
                    if cur:
                        pe.wait_ge(S["e1a"], i + 1)
                    project(r2, xq, w3s[:, 0, 0], w3s[:, 0, 1]).then_inc(S["r_mm"], 1)
                    project(r0, xq, w3s[:, 1, 0], w3s[:, 1, 1]).then_inc(S["p_mm"], 1)
                if nxt:
                    pe.wait_ge(S["y0_lo"], i + 2)
                    project(r1, yT, w0s[:, 0], w0s[:, 1]).then_inc(S["p0_mm"], 1)
                if prev:
                    pe.wait_ge(S["r_lo"], i)
                    project(r2, xq, w3s[:, 2, 0], w3s[:, 2, 1]).then_inc(S["u_mm"], 1)
                    pe.wait_ge(S["p_cp"], i)
                    if isinstance(i, int) and i == 1:
                        pe.wait_ge(S["lap_lo"], C)
                    apply_laplacian(r0, gr, 0, C - 1)
                if nxt:
                    pe.wait_ge(S["x1_ok"], i + 2)
                    transpose_nodes(r1, x1).then_inc(S["x1t_mm"], 1)
                if prev:
                    apply_laplacian(r0, gr, C - 1, C).then_inc(S["t_mm"], 1)
                if nxt:
                    pe.wait_ge(S["x1t_lo"], i + 2)
                    for h in range(2):
                        hs = slice(h * HALF, (h + 1) * HALF)
                        l_ = split_product(r2[:, hs], ms[:, 0], ms[:, 1], x1T[:, 0, hs], x1T[:, 1, hs], True, True)
                    l_.then_inc(S["g_mm"], 1)
                    project(r1, x1T, vs[:, 0], vs[:, 1]).then_inc(S["v_mm"], 1)
                if prev:
                    pe.wait_ge(S["q_lo"], i)
                    apply_laplacian(r0, xq, 0, C).then_inc(S["o_mm"], 1)

            iterations(pe, body)


_INS = ["x", "adj", "L0_gnn_weight", "L0_gnn_bias", "L1_gnn_q", "L1_gnn_k", "L1_gnn_v", "L2_gnn_g_w", "L2_gnn_g_b",
        "L2_gnn_weight", "L2_gnn_bias", "L3_gnn_weight", "L3_gnn_bias"]


def kernel(**inputs):
    import numpy as _np
    import concourse.bacc as _bacc
    from concourse import mybir as _mybir
    from concourse.bass_utils import run_bass_kernel_spmd as _run

    nc = _bacc.Bacc("TRN2", target_bir_lowering=False, num_devices=1)
    arrays, args = {}, []
    for name in _INS:
        a = _np.ascontiguousarray(inputs[name])
        if a.ndim == 0:
            a = a.reshape(1)
        arrays[f"in_{name}"] = a
        args.append(nc.dram_tensor(f"in_{name}", a.shape, _mybir.dt.from_np(a.dtype), kind="ExternalInput").ap())
    args.append(nc.dram_tensor("out_0", (B, N, D), _mybir.dt.float32, kind="ExternalOutput").ap())
    adj_resnorm(nc, *args)
    r = _run(nc, [arrays], core_ids=[0])
    return r.results[0]["out_0"]
```

```python
import concourse.bass as bass
from concourse import mybir
from contextlib import ExitStack
import numpy as np

F32 = mybir.dt.float32
F16 = mybir.dt.float16
U32 = mybir.dt.uint32
ALU = mybir.AluOpType
ACT = mybir.ActivationFunctionType
AX = mybir.AxisListType

B, N, D = 8, 1024, 128
P = 128
C = N // P
HALF = 512
EPS = 1e-5
NORM_FLOOR = 1e-12
MIN_MAX = 1e-30
POW2_MASK = 0x7F800000

X_UP = 16.0
SUM_UP = 4096.0
SJ_UP = 1024.0
W_DOWN = 1.0 / 32
Q_DOWN = 1.0 / 4
ADJ_UP = 256.0
LAP_UP = 64.0
LO_UP = 2048.0
P_UP = 16.0
Y0_DOWN = 1.0 / 1024
Y2_DOWN = 1.0 / 1024
TANH_CAP = 8.0
ROOT, ARG, SHIFT = 5, 6, 7
LN_ARG = 5
LN_LINKS = 6
L2_LINKS = 4
WEIGHTS_AT = 3
V_CHUNKS = 4
AVW = 130
RING = 4
AHEAD = 3


class Count:

    def __init__(self, eng, sem, b, per):
        self.eng, self.sem, self.base, self.per, self.n = eng, sem, b * per, per, 0

    def mark(self, ins):
        ins.then_inc(self.sem, 1)
        self.n += 1

    def wait(self):
        self.eng.wait_ge(self.sem, self.base + self.n)

    def link(self, ins):
        self.mark(ins)
        self.wait()

    def end(self):
        assert self.n == self.per, (self.n, self.per)


def adj_resnorm(nc, x, adj, w0, b0, q, k, v, gw, gb, w2, b2, w3, b3, out):
    ctx = ExitStack()
    with ctx:
        def sb(name, shape, dt=F32):
            return ctx.enter_context(nc.sbuf_tensor(name, shape, dt))

        def ps(name, shape):
            return ctx.enter_context(nc.psum_tensor(name, shape, F32))

        def sem(name):
            return ctx.enter_context(nc.semaphore(name))

        adjT = sb("adjT", [P, C, N])
        a_hi = sb("a_hi", [P, C, N], F16)
        a_lo = sb("a_lo", [P, C, N], F16)
        lap = sb("lap", [P, 2, C, N], F16)
        adj_rows = lap[:].rearrange("p a c n -> p (a c n)").bitcast(F32).rearrange("p (c n) -> p c n", c=C)
        ident = sb("ident", [P, P])
        ident_up = sb("ident_up", [P, P], F16)
        ones = sb("ones", [P, P])
        w2_sb = sb("w2_sb", [P, D])
        w0s, ms, vs, w2s = (sb(n_, [P, 2, D], F16) for n_ in ("w0s", "ms", "vs", "w2s"))
        w3s = sb("w3s", [P, 3, 2, D], F16)
        wjp = sb("wjp", [P, 4])
        b0_bc, b2_bc, b3_bc, wj_bc, wi_bc = (sb(n_, [P, D]) for n_ in ("b0_bc", "b2_bc", "b3_bc", "wj_bc", "wi_bc"))
        wr_gb = sb("wr_gb", [P, 2])
        wmax, wpow, winv = (sb(n_, [P, 5]) for n_ in ("wmax", "wpow", "winv"))
        coef = sb("coef", [P, 8])
        c_w0, c_tanh, c_v, c_l2, c_u, c_o = (coef[:, j:j + 1] for j in range(6))
        deg, dis = sb("deg", [P, C]), sb("dis", [P, C])
        x0 = sb("x0", [P, C, D])
        xmax, xpow, xinv, c_y0 = (sb(n_, [P, 1]) for n_ in ("xmax", "xpow", "xinv", "c_y0"))
        x0s = sb("x0s", [P, 2, C, D], F16)
        yT = sb("yT", [P, 2, N], F16)
        x1 = sb("x1", [P, C, D])
        x1T = sb("x1T", [P, 2, N], F16)
        gr = sb("gr", [P, 2, N], F16)
        vhi = sb("vhi", [P, C, AVW], F16)
        vlo = sb("vlo", [P, C, D], F16)
        vhs = sb("vhs", [P, C, AVW], F16)
        att = sb("att", [P, RING, N])
        p_hi, p_lo = sb("p_hi", [P, RING, N], F16), sb("p_lo", [P, RING, N], F16)
        x2 = sb("x2", [P, C, D])
        w0_sb, q_sb, k_sb, v_sb, qT, kT, m_sb = (x2[:, j] for j in range(7))
        x2s = sb("x2s", [P, 2, C, D], F16)
        one_sj = sb("one_sj", [P, C, 3], F16)
        sj = sb("sj", [P, C])
        sig = sb("sig", [P, C])
        tmp = sb("tmp", [P, C, D])
        xs = sb("xs", [P, 4])
        xb = sb("xb", [P, 2, P])
        r2b = sb("r2b", [P, D])
        x3 = sb("x3", [P, C, D])
        w3_sb, w3c = x3[:, 0:3], x3[:, 3:6]
        xq = sb("xq", [P, 2, N], F16)
        pq = sb("pq", [P, C, D])
        u = sb("u", [P, C, D])
        outb = sb("outb", [P, C, D])
        stats = sb("stats", [P, 5, C, 2, 3])
        pair = sb("pair", [P, C, 2])
        minus_half = sb("minus_half", [P, C])
        small = sb("small", [P, 5, 8, C])
        rsum, rinv = sb("rsum", [P, 9]), sb("rinv", [P, C])
        junk = att[:].rearrange("p r n -> p (r n)").bitcast(F16)
        dis_bc = pq[:].rearrange("p c d -> p (c d)")
        lap_f = u[:].rearrange("p c d -> p (c d)")
        lap_g = outb[:].rearrange("p c d -> p (c d)")

        r0 = ps("r0", [P, N])
        r1 = ps("r1", [P, N])
        av = ps("av", [P, 3, HALF])
        m7 = ps("m7", [P, HALF])
        r2 = av[:].rearrange("p a n -> p (a n)")[:, 0:N]

        def cd(ap):
            return ap.rearrange("p (c d) -> p c d", c=C)

        names = ("w_in wq_in x_in ident_ok const_ok qk_t qk_c m_cp m_mm w_max w_sum w_red w_ok wj_c "
                 "tr adj_hi adj_cp adj_lo deg_ok diag_ok dbc_mm lap_st lap_hi lap_lo "
                 "norm_r dis_ok x_max x_sum x_st x_hi x_lo "
                 "y0_mm y0_hi y0_lo p0_mm e0_c e0 x1t_mm x1t_hi x1t_lo g_mm g_hi g_lo v_mm v_hi v_s v_lo "
                 "s_mm th ex pm ph pl av_mm e1a e1a_c x2_hi sj_c e1b "
                 "xx_mm xb_c xb_ok y2_mm y2_hi y2_lo rr_mm p2_mm l2_c x3t_mm x3t_hi x3t_lo "
                 "r_mm r_hi r_lo p_mm p_cp u_mm u_ok t_mm q_ok q_hi q_lo o_mm fa f_c stored").split()
        names += [f"ln{k_}{end}" for k_ in range(4) for end in ("", "_r", "_v", "_a")]
        S = {n_: sem(n_) for n_ in names}
        adj_in = [sem(f"adj_in{c}") for c in range(C)]

        block = ctx.enter_context(nc.Block())

        def half(h):
            return slice(h * HALF, (h + 1) * HALF)

        def chunk(c):
            return slice(c * P, (c + 1) * P)

        def half_chunks(h):
            return slice(h * C // 2, (h + 1) * C // 2)

        def is_first(i, n):
            return isinstance(i, int) and i == n

        def iterations(eng, body):
            body(-1, True, False, False, False)
            body(0, True, True, False, False)
            body(1, True, True, True, False)
            body(2, True, True, True, True)
            with eng.Fori(3, B - 1) as i:
                body(i, True, True, True, True)
            body(B - 1, False, True, True, True)
            body(B, False, False, True, True)
            body(B + 1, False, False, False, True)

        x_v = x.rearrange("b (c p) d -> b p c d", p=P)

        @block.sync
        def _(sp):
            sp.dma_start(x0[:], x_v[0]).then_inc(S["x_in"], 16)
            adj_v = adj.rearrange("(c p) m -> c p m", p=P)
            for c in range(C):
                sp.dma_start(adj_rows[:, c, :], adj_v[c]).then_inc(adj_in[c], 16)
                if c == 1:
                    for dst, src in ((b0_bc[:], b0), (b2_bc[:], b2), (b3_bc[:], b3.rearrange("a b d -> (a b d)")),
                                     (wj_bc[:], gw[0:D]), (wi_bc[:], gw[D:2 * D]),
                                     (wr_gb[:, 0:1], gw[2 * D:2 * D + 1]), (wr_gb[:, 1:2], gb)):
                        sp.dma_start(dst, src.partition_broadcast(P)).then_inc(S["w_in"], 16)
            out_v = out.rearrange("b (c p) d -> b p c d", p=P)

            def body(i, nxt, cur, prev, last):
                if nxt and cur:
                    sp.wait_ge(S["e0"], i + 1)
                    sp.dma_start(x0[:], x_v[i + 1]).then_inc(S["x_in"], 16)
                if last:
                    sp.wait_ge(S["ln3_a"], i - 1)
                    sp.dma_start(out_v[i - 2], outb[:]).then_inc(S["stored"], 16)

            iterations(sp, body)
            sp.wait_ge(S["stored"], 16 * B)

        @block.gpsimd
        def _(pool):
            nc.gpsimd.memset(ident[:], 0.0).then_inc(S["ident_ok"], 1)
            pool.wait_ge(S["ident_ok"], 1)
            nc.gpsimd.affine_select(out=ident[:], in_=ident[:], compare_op=ALU.not_equal, fill=1.0, base=0,
                                    pattern=[[-1, P]], channel_multiplier=1).then_inc(S["ident_ok"], 1)
            nc.gpsimd.memset(minus_half[:], -0.5).then_inc(S["ident_ok"], 1)
            pool.wait_ge(S["ident_ok"], 3)

            def inverse_root(dst, src):
                return nc.gpsimd.tensor_tensor(dst, src, minus_half[:], ALU.pow)

            def norm_root(k_, b):
                pool.wait_ge(S[f"ln{k_}"], LN_LINKS * b + LN_ARG)
                inverse_root(small[:, k_, ROOT], small[:, k_, ARG]).then_inc(S[f"ln{k_}_r"], 1)

            def body(i, nxt, cur, prev, last):
                if prev:
                    norm_root(2, i - 1)
                if last:
                    norm_root(3, i - 2)
                if is_first(i, 0):
                    norm_root(1, i)
                if is_first(i, -1):
                    pool.wait_ge(S["deg_ok"], C)
                    inverse_root(dis[:], deg[:]).then_inc(S["dis_ok"], 1)
                if nxt:
                    pool.wait_ge(S["e0_c"], 8 * (i + 2))
                    inverse_root(small[:, 4, ROOT], small[:, 4, ARG]).then_inc(S["norm_r"], 1)
                if nxt:
                    norm_root(0, i + 1)
                if prev and cur:
                    norm_root(1, i)

            iterations(pool, body)

        @block.scalar
        def _(act):
            for dst, src in ((q_sb, q), (k_sb, k)):
                act.dma_start(dst, src).then_inc(S["wq_in"], 16)
            for dst, src in ((w0_sb, w0), (v_sb, v), (w2_sb[:], w2)):
                act.dma_start(dst, src).then_inc(S["w_in"], 16)
            act.dma_start(w3_sb, w3.rearrange("k o c d -> c (k o) d")).then_inc(S["w_in"], 16)

            def copy(dst, src, scale=1.0, **more):
                return nc.scalar.activation(dst, src, ACT.Copy, scale=scale, **more)

            def x0_hi(b):
                act.wait_ge(S["x_st"], 5 * (b + 1))
                copy(x0s[:, 0], x0[:], xinv[:]).then_inc(S["x_hi"], 1)

            x0_hi(0)
            for c in range(C):
                act.wait_ge(S["tr"], c + 1)
                src = cd((r0[:], r2)[c % 2])
                copy(a_hi[:, :, chunk(c)], src, ADJ_UP).then_inc(S["adj_hi"], 1)
                copy(adjT[:, :, chunk(c)], src, LO_UP * P_UP).then_inc(S["adj_cp"], 1)

            def degrees(first, last_):
                for c in range(first, last_):
                    copy(junk[:, c * N:(c + 1) * N], adj_rows[:, c, :], accum_out=deg[:, c:c + 1]).then_inc(S["deg_ok"], 1)

            def lap_hi_part(*rows):
                for c in rows:
                    act.wait_ge(S["lap_st"], 2 * (c + 1))
                    copy(lap[:, 0, c, :], (lap_f, lap_g)[c % 2]).then_inc(S["lap_hi"], 1)

            def norm(k_, b, t, first):
                act.wait_ge(S[f"ln{k_}"], LN_LINKS * (b + 1))
                for j in range(first, C):
                    l_ = nc.scalar.activation(t[:, j], t[:, j], ACT.Identity, scale=small[:, k_, ROOT, j:j + 1],
                                              bias=small[:, k_, SHIFT, j:j + 1])
                l_.then_inc(S[f"ln{k_}_a"], 1)

            def body(i, nxt, cur, prev, last):
                t8 = i * C

                def y2_half(h):
                    act.wait_ge(S["y2_mm"], 2 * (i - 1) + h + 1)
                    if h == 0:
                        act.wait_ge(S["p0_mm"], 2 * (i + 1 if cur or nxt else B))
                    copy(yT[:, 0, half(h)], m7[:], Y2_DOWN).then_inc(S["y2_hi"], 1)

                def y0_half(h):
                    act.wait_ge(S["y0_mm"], 2 * (i + 1) + h + 1)
                    if prev and h == 0:
                        act.wait_ge(S["p2_mm"], i)
                    copy(yT[:, 0, half(h)], r1[:, half(h)], Y0_DOWN).then_inc(S["y0_hi"], 1)

                def copy_x2():
                    act.wait_ge(S["ln1_v"], i + 1)
                    act.wait_ge(S["ln1_a"], i + 1)
                    if prev:
                        act.wait_ge(S["y2_mm"], 2 * i)
                    copy(x2s[:, 0], x2[:], X_UP).then_inc(S["x2_hi"], 1)

                def p_hi_part(t):
                    act.wait_ge(S["pm"], t8 + t + 1)
                    if not (is_first(i, 0) and t < RING):
                        act.wait_ge(S["av_mm"], t8 + t - RING + 1)
                    s = t % RING
                    copy(p_hi[:, s], att[:, s], 1.0 / LO_UP).then_inc(S["ph"], 1)

                if cur:
                    for t in range(C):
                        s = t % RING
                        act.wait_ge(S["s_mm"], t8 + t + 1)
                        if not (is_first(i, 0) and t < RING):
                            act.wait_ge(S["pl"], t8 + t - RING + 1)
                        nc.scalar.activation(att[:, s], (r1, r0)[t % 2][:], ACT.Tanh, scale=c_tanh).then_inc(S["th"], 1)
                        act.wait_ge(S["th"], t8 + t + 1)
                        nc.scalar.activation(att[:, s], att[:, s], ACT.Exp, scale=TANH_CAP).then_inc(S["ex"], 1)
                        if t >= 1:
                            p_hi_part(t - 1)
                        if t == 5 and prev:
                            y2_half(0)
                        if is_first(i, 1) and t in (2, 3, 4):
                            lap_hi_part(t + 3)
                    p_hi_part(C - 1)
                elif prev:
                    y2_half(0)
                if nxt and cur:
                    act.wait_ge(S["y0_mm"], 2 * (i + 1))
                    x0_hi(i + 1)
                if prev:
                    y2_half(1)
                if is_first(i, 0):
                    lap_hi_part(2)
                if nxt:
                    y0_half(0)
                if is_first(i, 0):
                    norm(1, i, x2, V_CHUNKS)
                if prev:
                    norm(2, i - 1, x3, V_CHUNKS)
                if is_first(i, -1):
                    degrees(0, 5)
                if nxt:
                    y0_half(1)
                if is_first(i, -1):
                    degrees(5, C)
                if is_first(i, 0):
                    lap_hi_part(3, 4)
                    copy_x2()
                if prev:
                    for h in range(2):
                        act.wait_ge(S["x3t_mm"], 2 * (i - 1) + h + 1)
                        if last and h == 0:
                            act.wait_ge(S["o_mm"], i - 1)
                        copy(xq[:, 0, half(h)], r0[:, half(h)], X_UP).then_inc(S["x3t_hi"], 1)
                    for h in range(2):
                        act.wait_ge(S["r_mm"], 2 * (i - 1) + h + 1)
                        copy(gr[:, 0, half(h)], r2[:, half(h)], W_DOWN).then_inc(S["r_hi"], 1)
                    act.wait_ge(S["p_mm"], i)
                    if last:
                        act.wait_ge(S["q_lo"], 2 * (i - 1))
                    if is_first(i, 1):
                        act.wait_ge(S["lap_st"], 2 * C)
                    copy(pq[:], cd(r0[:]), W_DOWN * Q_DOWN).then_inc(S["p_cp"], 1)
                if last:
                    norm(3, i - 2, outb, 0)

                def q_hi(h):
                    act.wait_ge(S["q_ok"], 2 * (i - 1) + h + 1)
                    if h == 0:
                        act.wait_ge(S["u_mm"], i)
                    copy(cd(xq[:, 0])[:, half_chunks(h)], pq[:, half_chunks(h)]).then_inc(S["q_hi"], 1)

                if prev:
                    q_hi(0)
                if nxt:
                    norm(0, i + 1, x1, V_CHUNKS)
                    for h in range(2):
                        act.wait_ge(S["x1t_mm"], 2 * (i + 1) + h + 1)
                        copy(x1T[:, 0, half(h)], r1[:, half(h)], X_UP).then_inc(S["x1t_hi"], 1)
                if is_first(i, -1):
                    lap_hi_part(0)
                if prev and cur:
                    norm(1, i, x2, V_CHUNKS)
                if prev:
                    q_hi(1)
                if nxt:
                    for h in range(2):
                        act.wait_ge(S["g_mm"], 2 * (i + 1) + h + 1)
                        if prev and h == 0:
                            act.wait_ge(S["t_mm"], 2 * i)
                        copy(gr[:, 0, half(h)], r2[:, half(h)], W_DOWN).then_inc(S["g_hi"], 1)
                    if is_first(i, -1):
                        lap_hi_part(1)
                    for h in range(2):
                        act.wait_ge(S["v_mm"], 2 * (i + 1) + h + 1)
                        if cur and h == 0:
                            act.wait_ge(S["av_mm"], C * (i + 1))
                        copy(vhi[:, half_chunks(h), 0:D], cd(r1[:])[:, half_chunks(h)], W_DOWN).then_inc(S["v_hi"], 1)
                    act.wait_ge(S["v_hi"], 2 * (i + 2))
                    copy(vhs[:, :, 0:D], vhi[:, :, 0:D], 1.0 / LO_UP).then_inc(S["v_s"], 1)
                if prev and cur:
                    copy_x2()

            iterations(act, body)

        @block.vector
        def _(dve):
            tt = nc.vector.tensor_tensor
            ts = nc.vector.tensor_scalar
            stt = nc.vector.scalar_tensor_tensor

            def row(ap, n=C):
                return ap.unsqueeze(1).to_broadcast([P, n, D])

            def chunk_stats(k_, src, chunks=range(C)):
                for j in chunks:
                    l_ = nc.vector.bn_stats(stats[:, k_, j].rearrange("p a k -> p (a k)"), src[:, j])
                return l_

            def ln_stats(k_, b, src):
                chunk_stats(k_, src).then_inc(S[f"ln{k_}"], 1)

            def ln_arg(k_, b):
                ch = Count(dve, S[f"ln{k_}"], b, LN_ARG)
                ch.base, ch.n = LN_LINKS * b, 1
                ch.wait()
                st, sm = stats[:, k_], small[:, k_]
                me, mo = st[:, :, 0, 1], st[:, :, 1, 1]
                tt(sm[:, 0], me, mo, ALU.add)
                tt(sm[:, 1], me, mo, ALU.subtract)
                ch.link(tt(sm[:, 2], st[:, :, 0, 2], st[:, :, 1, 2], ALU.add))
                tt(sm[:, 3], sm[:, 1], sm[:, 1], ALU.mult)
                ch.link(ts(sm[:, 4], sm[:, 0], -0.5, None, ALU.mult))
                ch.link(stt(sm[:, 0], sm[:, 3], D / 4.0, sm[:, 2], ALU.mult, ALU.add))
                ch.mark(ts(sm[:, ARG], sm[:, 0], 1.0 / D, EPS, ALU.mult, ALU.add))
                ch.end()

            def ln_begin(k_, b, src):
                ln_stats(k_, b, src)
                ln_arg(k_, b)

            def ln_shift(k_, b):
                dve.wait_ge(S[f"ln{k_}_r"], b + 1)
                sm = small[:, k_]
                tt(sm[:, SHIFT], sm[:, 4], sm[:, ROOT], ALU.mult).then_inc(S[f"ln{k_}"], 1)

            def ln_norm(k_, b, t):
                dve.wait_ge(S[f"ln{k_}"], LN_LINKS * (b + 1))
                sm = small[:, k_]
                for j in range(V_CHUNKS):
                    l_ = ts(t[:, j], t[:, j], sm[:, ROOT, j:j + 1], sm[:, SHIFT, j:j + 1], ALU.mult, ALU.add)
                l_.then_inc(S[f"ln{k_}_v"], 1)

            nc.vector.memset(ones[:], 1.0)
            nc.vector.memset(one_sj[:, :, 0:1], 1.0)
            nc.vector.memset(vhi[:, :, D:D + 1], 1.0)
            nc.vector.memset(vhs[:, :, D:D + 1], 1.0 / LO_UP).then_inc(S["const_ok"], 1)

            def x0_max(b):
                dve.wait_ge(S["x_in"], 16 * (b + 1))
                nc.vector.tensor_reduce(xmax[:], x0[:].rearrange("p c d -> p (c d)"), AX.X, ALU.max,
                                        apply_absolute_value=True).then_inc(S["x_max"], 1)

            def x0_scale_read(b):
                dve.wait_ge(S["x_sum"], b + 1)
                ts(xpow[:], m7[:, 4:5], MIN_MAX, None, ALU.max).then_inc(S["x_st"], 1)

            def x0_scales(b):
                ch = Count(dve, S["x_st"], b, 5)
                ch.n = 1
                ch.wait()
                ch.link(ts(xpow[:].bitcast(U32), xpow[:].bitcast(U32), POW2_MASK, None, ALU.bitwise_and))
                ch.link(nc.vector.reciprocal(xinv[:], xpow[:]))
                ch.mark(ts(c_y0[:], xpow[:], 1.0 / SUM_UP, None, ALU.mult))
                ch.mark(ts(xinv[:], xinv[:], SUM_UP, None, ALU.mult))
                ch.end()

            def x0_lo(b):
                dve.wait_ge(S["x_hi"], b + 1)
                stt(x0s[:, 1], x0[:], xinv[:], x0s[:, 0], ALU.mult, ALU.subtract).then_inc(S["x_lo"], 1)

            x0_max(0)
            dve.wait_ge(S["qk_t"], 1)
            nc.vector.tensor_copy(qT, m7[:, 0:P])
            nc.vector.tensor_copy(kT, m7[:, P:2 * P]).then_inc(S["qk_c"], 1)
            dve.wait_ge(S["m_mm"], 1)
            nc.vector.tensor_copy(m_sb, m7[:, 2 * P:3 * P]).then_inc(S["m_cp"], 1)
            x0_scale_read(0)
            x0_scales(0)
            x0_lo(0)

            def weights_max():
                dve.wait_ge(S["w_in"], 16 * 11)
                tt(w3c[:, 2], w3_sb[:, 0], w3_sb[:, 2], ALU.subtract)
                nc.vector.tensor_copy(w3c[:, 0], w3_sb[:, 2])
                nc.vector.tensor_copy(w3c[:, 1], w3_sb[:, 1]).then_inc(S["m_cp"], 1)
                dve.wait_ge(S["m_cp"], 2)
                for j, w in enumerate((w0_sb, m_sb, v_sb, w2_sb[:], w3c.rearrange("p k d -> p (k d)"))):
                    nc.vector.tensor_reduce(wmax[:, j:j + 1], w, AX.X, ALU.max,
                                            apply_absolute_value=True).then_inc(S["w_max"], 1)

            def weights():
                ch = Count(dve, S["wj_c"], 0, 6)
                ch.link(nc.vector.tensor_reduce(wjp[:, 0:1], wj_bc[:], AX.X, ALU.add, apply_absolute_value=True))
                ch.link(ts(wjp[:, 1:2], wjp[:, 0:1], MIN_MAX, None, ALU.max))
                ch.link(ts(wjp[:, 1:2].bitcast(U32), wjp[:, 1:2].bitcast(U32), POW2_MASK, None, ALU.bitwise_and))
                ts(wjp[:, 3:4], wjp[:, 1:2], 1.0 / (X_UP * SJ_UP), None, ALU.mult)
                ch.link(nc.vector.reciprocal(wjp[:, 2:3], wjp[:, 1:2]))
                ch.link(ts(wjp[:, 2:3], wjp[:, 2:3], SJ_UP, None, ALU.mult))
                ch.link(ts(wj_bc[:], wj_bc[:], wjp[:, 2:3], None, ALU.mult))
                ch.end()
                dve.wait_ge(S["w_sum"], 1)
                ch = Count(dve, S["w_red"], 0, 12)
                ch.link(ts(wpow[:], m7[:, 3 * P:3 * P + 5], MIN_MAX, None, ALU.max))
                ch.link(ts(wpow[:].bitcast(U32), wpow[:].bitcast(U32), POW2_MASK, None, ALU.bitwise_and))
                ch.link(nc.vector.reciprocal(winv[:], wpow[:]))
                ch.link(ts(winv[:], winv[:], SUM_UP, None, ALU.mult))
                parts = ((w0_sb, w0s[:, 0], w0s[:, 1]), (m_sb, ms[:, 0], ms[:, 1]),
                         (v_sb, vs[:, 0], vs[:, 1]), (w2_sb[:], w2s[:, 0], w2s[:, 1]),
                         (w3c, w3s[:, :, 0], w3s[:, :, 1]))
                for j, (w, hi, lo) in enumerate(parts):
                    ch.link(ts(hi, w, winv[:, j:j + 1], None, ALU.mult))
                    l_ = stt(lo, w, winv[:, j:j + 1], hi, ALU.mult, ALU.subtract)
                ch.mark(l_)
                xw = X_UP * SUM_UP
                ts(c_w0, wpow[:, 0:1], 1.0 / (ADJ_UP * Y0_DOWN * SUM_UP), None, ALU.mult)
                ts(c_tanh, wpow[:, 1:2], 1.0 / (X_UP * xw * W_DOWN * float(np.sqrt(float(D))) * TANH_CAP), None, ALU.mult)
                ts(c_v, wpow[:, 2:3], 1.0 / (xw * W_DOWN), None, ALU.mult)
                ts(c_u, wpow[:, 4:5], 1.0 / xw, None, ALU.mult)
                ts(c_o, wpow[:, 4:5], 1.0 / (xw * W_DOWN * Q_DOWN * LAP_UP), None, ALU.mult)
                ch.link(ts(c_l2, wpow[:, 3:4], 1.0 / (xw * ADJ_UP * Y2_DOWN), None, ALU.mult))
                ch.link(ts(c_l2, c_l2, wr_gb[:, 0:1], None, ALU.mult))
                ch.end()

            for c in range(C):
                dve.wait_ge(S["adj_cp"], c + 1)
                stt(a_lo[:, :, chunk(c)], adjT[:, :, chunk(c)], ADJ_UP / (LO_UP * P_UP), a_hi[:, :, chunk(c)],
                    ALU.mult, ALU.subtract).then_inc(S["adj_lo"], 1)
                if c == WEIGHTS_AT - 2:
                    weights_max()
                if c == WEIGHTS_AT:
                    weights()
                if c == 0:
                    dve.wait_ge(S["ident_ok"], 3)
                    ts(ident_up[:], ident[:], ADJ_UP, None, ALU.mult).then_inc(S["adj_lo"], 1)

            def lap_row(*rows):
                for c in rows:
                    f = (lap_f, lap_g)[c % 2]
                    if c >= 2:
                        dve.wait_ge(S["lap_lo"], c - 1)
                    stt(f, adjT[:, c, :], dis[:, c:c + 1], dis_bc, ALU.mult, ALU.mult).then_inc(S["lap_st"], 1)
                    dve.wait_ge(S["lap_st"], 2 * c + 1)
                    stt(f[:, chunk(c)], ident[:], LAP_UP, f[:, chunk(c)], ALU.mult, ALU.add).then_inc(S["lap_st"], 1)

            def lap_lo_part(*rows):
                for c in rows:
                    dve.wait_ge(S["lap_hi"], c + 1)
                    tt(lap[:, 1, c, :], (lap_f, lap_g)[c % 2], lap[:, 0, c, :], ALU.subtract).then_inc(S["lap_lo"], 1)

            def body(i, nxt, cur, prev, last):
                t8 = i * C

                def split_lo(dst, src, scale, hi, name, count):
                    dve.wait_ge(S[name + "_hi"], count)
                    stt(dst, src, scale, hi, ALU.mult, ALU.subtract).then_inc(S[name + "_lo"], 1)

                def mask(t):
                    dve.wait_ge(S["ex"], t8 + t + 1)
                    s = t % RING
                    tt(att[:, s], att[:, s], adjT[:, t, :], ALU.mult).then_inc(S["pm"], 1)

                def p_lo_part(t):
                    dve.wait_ge(S["ph"], t8 + t + 1)
                    s = t % RING
                    stt(p_lo[:, s], p_hi[:, s], -LO_UP, att[:, s], ALU.mult, ALU.add).then_inc(S["pl"], 1)

                def y2_half(h):
                    split_lo(yT[:, 1, half(h)], m7[:], Y2_DOWN, yT[:, 0, half(h)], "y2", 2 * (i - 1) + h + 1)

                def sums_read():
                    dve.wait_ge(S["xx_mm"], i)
                    nc.vector.tensor_copy(xs[:, 0:3], m7[:, 0:3]).then_inc(S["xb_c"], 1)

                def sums():
                    ch = Count(dve, S["xb_c"], i - 1, 2)
                    ch.n = 1
                    ch.wait()
                    ts(xb[:, 0], xs[:, 0:1].to_broadcast([P, P]), 1.0 / X_UP, None, ALU.mult)
                    ch.link(tt(xs[:, 3:4], xs[:, 1:2], xs[:, 2:3], ALU.add))
                    ch.end()
                    ts(xb[:, 1], xs[:, 3:4].to_broadcast([P, P]), wjp[:, 3:4], None, ALU.mult).then_inc(S["xb_ok"], 1)

                if prev:
                    l2_ch = Count(dve, S["l2_c"], i - 1, L2_LINKS)

                def l2_read():
                    dve.wait_ge(S["rr_mm"], i)
                    nc.vector.tensor_copy(tmp[:, 0], m7[:, 0:P])
                    l2_ch.mark(tt(r2b[:], m7[:, P:2 * P], b2_bc[:], ALU.add))

                def l2_rank_one():
                    l2_ch.wait()
                    if last:
                        dve.wait_ge(S["f_c"], i - 1)
                    for j in range(C):
                        l_ = stt(x3[:, j], tmp[:, 0], sig[:, j:j + 1], x2[:, j], ALU.mult, ALU.add)
                    l2_ch.mark(l_)

                def l2_row():
                    l2_ch.wait()
                    l2_ch.link(tt(x3[:], x3[:], row(r2b[:]), ALU.add))

                if cur:
                    sj_ch = Count(dve, S["sj_c"], i, 5)

                def sj_step(step):
                    ch = sj_ch
                    if step == 0:
                        dve.wait_ge(S["ln1_a"], i + 1)
                        dve.wait_ge(S["ln1_v"], i + 1)
                        ch.link(tt(tmp[:], x2[:], row(wj_bc[:]), ALU.mult))
                    if step == 1:
                        ch.link(nc.vector.tensor_reduce(sj[:], tmp[:], AX.X, ALU.add))
                        nc.vector.tensor_copy(one_sj[:, :, 1], sj[:])
                    if step == 2:
                        ch.link(tt(tmp[:], x2[:], row(wi_bc[:]), ALU.mult))
                        tt(one_sj[:, :, 2], sj[:], one_sj[:, :, 1], ALU.subtract)
                    if step == 3:
                        ch.link(nc.vector.tensor_reduce(sig[:], tmp[:], AX.X, ALU.add))
                        ch.link(ts(sig[:], sig[:], wr_gb[:, 1:2], None, ALU.add))
                        ch.end()
                        dve.wait_ge(S["x2_hi"], i + 1)
                        stt(x2s[:, 1], x2[:], X_UP, x2s[:, 0], ALU.mult, ALU.subtract).then_inc(S["e1b"], 1)

                def relu_residual():
                    dve.wait_ge(S["fa"], i - 1)
                    if not is_first(i, 2):
                        dve.wait_ge(S["stored"], 16 * (i - 2))
                    stt(outb[:], u[:], 0.0, x3[:], ALU.max, ALU.add).then_inc(S["f_c"], 1)

                def finish_stats():
                    dve.wait_ge(S["f_c"], i - 1)
                    ln_stats(3, i - 2, outb)

                if nxt and cur:
                    x0_max(i + 1)
                if last:
                    dve.wait_ge(S["o_mm"], i - 1)
                    stt(u[:], cd(r0[:]), c_o, u[:], ALU.mult, ALU.add).then_inc(S["fa"], 1)
                if prev:
                    sums_read()
                if nxt and cur:
                    x0_scale_read(i + 1)
                if prev:
                    sums()
                if cur:
                    mask(0)
                if prev and cur:
                    l2_read()
                if nxt and cur:
                    x0_scales(i + 1)
                if cur:
                    for t in range(1, C):
                        mask(t)
                        p_lo_part(t - 1)
                        if prev and t == 4:
                            l2_rank_one()
                        if prev and t == 6:
                            l2_row()
                        if t == 3 and last:
                            relu_residual()
                        if t == 5 and prev:
                            y2_half(0)
                        if is_first(i, 1) and t in (2, 3, 4):
                            lap_lo_part(t + 3)
                        if is_first(i, 1) and t in (1, 2, 3):
                            lap_row(t + 4)
                    p_lo_part(C - 1)
                    if nxt:
                        x0_lo(i + 1)
                else:
                    if prev:
                        l2_read()
                    if last:
                        relu_residual()
                    if prev:
                        y2_half(0)
                        l2_rank_one()
                        l2_row()

                def y0_half(h):
                    split_lo(yT[:, 1, half(h)], r1[:, half(h)], Y0_DOWN, yT[:, 0, half(h)], "y0", 2 * (i + 1) + h + 1)

                if prev:
                    y2_half(1)
                if last:
                    finish_stats()
                if prev:
                    dve.wait_ge(S["p2_mm"], i)
                    l2_ch.link(stt(x3[:], cd(r0[:]), c_l2, x3[:], ALU.mult, ALU.add))
                    l2_ch.end()
                    ln_begin(2, i - 1, x3)
                if last:
                    ln_arg(3, i - 2)
                if cur:
                    ch = Count(dve, S["e1a_c"], i, 2)
                    dve.wait_ge(S["av_mm"], C * (i + 1))
                    for k_ in range(3):
                        w = min(3, C - 3 * k_)
                        l_ = nc.vector.reciprocal(rsum[:, 3 * k_:3 * k_ + w], av[:, k_, D:D + AVW * (w - 1) + 1:AVW])
                    ch.link(l_)
                    ch.link(ts(rinv[:], rsum[:, 0:C], c_v, None, ALU.mult))
                    ch.end()
                    if prev and nxt:
                        y0_half(0)
                    for j in range(C):
                        o = (j % 3) * AVW
                        l_ = stt(x2[:, j], av[:, j // 3, o:o + D], rinv[:, j:j + 1], x1[:, j], ALU.mult, ALU.add)
                        if prev and j == C // 2:
                            ln_shift(2, i - 1)
                    l_.then_inc(S["e1a"], 1)
                elif prev:
                    ln_shift(2, i - 1)
                if prev:
                    ln_norm(2, i - 1, x3)
                if last:
                    ln_shift(3, i - 2)
                if is_first(i, 0):
                    dve.wait_ge(S["e1a"], i + 1)
                    ln_begin(1, i, x2)
                    y0_half(0)
                    ln_shift(1, i)
                    ln_norm(1, i, x2)
                    lap_row(3)
                    lap_lo_part(2)
                    lap_row(4)
                if nxt and not cur:
                    y0_half(0)
                if nxt:
                    c_y = small[:, 4, 2, 0:1]
                    ch = Count(dve, S["e0_c"], i + 1, 8)
                    ch.link(ts(c_y, c_y0[:], c_w0, None, ALU.mult))

                    def y_half(h):
                        hc = half_chunks(h)
                        dve.wait_ge(S["p0_mm"], 2 * (i + 1) + h + 1)
                        return stt(x1[:, hc], cd(r1[:])[:, hc], c_y, row(b0_bc[:], C // 2), ALU.mult, ALU.add)

                    if cur:
                        ch.link(y_half(0))
                        chunk_stats(4, x1, range(C // 2))
                        y0_half(1)
                    else:
                        y0_half(1)
                        ch.link(y_half(0))
                        chunk_stats(4, x1, range(C // 2))
                if prev:
                    for h in range(2):
                        split_lo(xq[:, 1, half(h)], r0[:, half(h)], X_UP, xq[:, 0, half(h)], "x3t", 2 * (i - 1) + h + 1)

                def r_half(h):
                    split_lo(gr[:, 1, half(h)], r2[:, half(h)], W_DOWN, gr[:, 0, half(h)], "r", 2 * (i - 1) + h + 1)


                def u_part():
                    dve.wait_ge(S["u_mm"], i)
                    stt(u[:], cd(r2), c_u, row(b3_bc[:]), ALU.mult, ALU.add).then_inc(S["u_ok"], 1)

                def q_part(h):
                    hc = half_chunks(h)
                    dve.wait_ge(S["t_mm"], 2 * (i - 1) + h + 1)
                    dve.wait_ge(S["p_cp"], i)
                    stt(pq[:, hc], cd(r0[:])[:, hc], 2.0 * Q_DOWN / LAP_UP, pq[:, hc], ALU.mult, ALU.add).then_inc(S["q_ok"], 1)

                def q_lo(h):
                    hc = half_chunks(h)
                    dve.wait_ge(S["q_hi"], 2 * (i - 1) + h + 1)
                    tt(cd(xq[:, 1])[:, hc], pq[:, hc], cd(xq[:, 0])[:, hc], ALU.subtract).then_inc(S["q_lo"], 1)

                if nxt:
                    ch.link(y_half(1))
                    if prev:
                        r_half(0)
                        r_half(1)
                    ch.link(chunk_stats(4, x1, range(C // 2, C)))
                    ch.link(tt(pair[:], stats[:, 4, :, :, 1], stats[:, 4, :, :, 1], ALU.mult))
                    ch.link(stt(pair[:], pair[:], D / 2.0, stats[:, 4, :, :, 2], ALU.mult, ALU.add))
                    ch.link(tt(small[:, 4, 0], pair[:, :, 0], pair[:, :, 1], ALU.add))
                    ch.mark(ts(small[:, 4, ARG], small[:, 4, 0], NORM_FLOOR * NORM_FLOOR, None, ALU.max))
                    ch.end()
                elif prev:
                    r_half(0)
                    r_half(1)
                if prev and cur:
                    dve.wait_ge(S["e1a"], i + 1)
                    ln_stats(1, i, x2)
                if cur and not nxt:
                    ln_arg(1, i)
                if is_first(i, 0):
                    lap_lo_part(3)
                if is_first(i, -1):
                    dve.wait_ge(S["dis_ok"], 1)
                    for c in range(C):
                        l_ = ts(tmp[:, c], ident[:], dis[:, c:c + 1], None, ALU.mult)
                    l_.then_inc(S["diag_ok"], 1)
                if nxt:
                    dve.wait_ge(S["norm_r"], i + 2)
                    for j in range(C):
                        l_ = stt(x1[:, j], x1[:, j], small[:, 4, ROOT, j:j + 1], x0[:, j], ALU.mult, ALU.add)
                    l_.then_inc(S["e0"], 1)
                    dve.wait_ge(S["e0"], i + 2)
                    ln_begin(0, i + 1, x1)
                if prev and cur and nxt:
                    ln_arg(1, i)
                if is_first(i, 0):
                    sj_step(0)
                if is_first(i, -1):
                    dve.wait_ge(S["dbc_mm"], 1)
                    ts(dis_bc, r0[:], -LAP_UP / (LO_UP * P_UP), None, ALU.mult).then_inc(S["diag_ok"], 1)
                    dve.wait_ge(S["diag_ok"], 2)
                if prev:
                    q_part(0)
                if nxt:
                    ln_shift(0, i + 1)
                    ln_norm(0, i + 1, x1)
                if prev and cur:
                    ln_shift(1, i)
                if prev:
                    q_lo(0)
                    u_part()
                if is_first(i, 0):
                    sj_step(1)
                if is_first(i, -1):
                    lap_row(0)

                def x1t_half(h):
                    split_lo(x1T[:, 1, half(h)], r1[:, half(h)], X_UP, x1T[:, 0, half(h)], "x1t", 2 * (i + 1) + h + 1)

                if nxt:
                    x1t_half(0)
                    x1t_half(1)
                if is_first(i, -1):
                    lap_row(1)
                if is_first(i, 0):
                    sj_step(2)
                if prev:
                    q_part(1)
                    if cur:
                        ln_norm(1, i, x2)
                    q_lo(1)
                if nxt:
                    for h in range(2):
                        split_lo(gr[:, 1, half(h)], r2[:, half(h)], W_DOWN, gr[:, 0, half(h)], "g", 2 * (i + 1) + h + 1)
                if is_first(i, -1):
                    lap_lo_part(0)
                if nxt:
                    for h in range(2):
                        hc = half_chunks(h)
                        split_lo(vlo[:, hc], cd(r1[:])[:, hc], W_DOWN, vhi[:, hc, 0:D], "v", 2 * (i + 1) + h + 1)
                if is_first(i, -1):
                    lap_lo_part(1)
                    lap_row(2)
                if is_first(i, 0):
                    sj_step(3)
                    lap_lo_part(4)
                elif cur:
                    for k_ in range(4):
                        sj_step(k_)

            iterations(dve, body)

        @block.tensor
        def _(pe):
            mm = nc.tensor.matmul

            pe.wait_ge(S["ident_ok"], 3)
            pe.wait_ge(S["wq_in"], 32)
            nc.tensor.transpose(m7[:, 0:P], q_sb, ident[:])
            nc.tensor.transpose(m7[:, P:2 * P], k_sb, ident[:]).then_inc(S["qk_t"], 1)
            pe.wait_ge(S["qk_c"], 1)
            pe.wait_ge(S["x_max"], 1)
            pe.wait_ge(S["const_ok"], 1)
            mm(m7[:, 4:5], ones[:], xmax[:], start=True, stop=True).then_inc(S["x_sum"], 1)
            mm(m7[:, 2 * P:3 * P], qT, kT, start=True, stop=True).then_inc(S["m_mm"], 1)
            def split_product(dst, s_hi, s_lo, m_hi, m_lo, start, stop):
                mm(dst, s_hi, m_hi, start=start, stop=False, skip_group_check=True)
                mm(dst, s_hi, m_lo, start=False, stop=False, skip_group_check=True)
                return mm(dst, s_lo, m_hi, start=False, stop=stop, skip_group_check=True)

            def transpose_half(dst, src, h):
                for j in range(h * C // 2, (h + 1) * C // 2):
                    l_ = nc.tensor.transpose(dst[:, chunk(j)], src[:, j], ident[:])
                return l_

            def project_half(dst, srcT, w_hi, w_lo, h):
                for j in range(h * C // 2, (h + 1) * C // 2):
                    l_ = split_product(dst[:, chunk(j)], srcT[:, 0, chunk(j)], srcT[:, 1, chunk(j)], w_hi, w_lo, True, True)
                return l_

            def project(dst, srcT, w_hi, w_lo):
                project_half(dst, srcT, w_hi, w_lo, 0)
                return project_half(dst, srcT, w_hi, w_lo, 1)

            def apply_laplacian(dst, src, first, last_):
                for j in range(first, last_):
                    for m in range(C):
                        l_ = split_product(dst[:, chunk(j)], lap[:, 0, m, chunk(j)], lap[:, 1, m, chunk(j)],
                                           src[:, 0, chunk(m)], src[:, 1, chunk(m)], m == 0, m == C - 1)
                return l_

            def adj_x0(h, first=0, last_=C):
                own = [m for m in range(C) if m // (C // 2) == h]
                order = own + [m for m in range(C) if m not in own]
                for n_ in range(first, last_):
                    m = order[n_]
                    l_ = split_product(r1[:, half(h)], x0s[:, 0, m], x0s[:, 1, m], a_hi[:, m, half(h)],
                                       a_lo[:, m, half(h)], n_ == 0, n_ == C - 1)
                    if m in own:
                        for part in range(2):
                            mm(r1[:, chunk(m)], x0s[:, part, m], ident_up[:], start=False, stop=False,
                               skip_group_check=True)
                if last_ == C:
                    l_.then_inc(S["y0_mm"], 1)

            for c in range(C):
                pe.wait_ge(adj_in[c], 16)
                if c >= 2:
                    pe.wait_ge(S["adj_cp"], c - 1)
                buf = (r0[:], r2)[c % 2]
                for m in range(C):
                    l_ = nc.tensor.transpose(buf[:, chunk(m)], adj_rows[:, c, chunk(m)], ident[:])
                l_.then_inc(S["tr"], 1)
                if c == WEIGHTS_AT:
                    pe.wait_ge(S["m_cp"], 1)
                    pe.wait_ge(S["x_st"], 1)
                    pe.wait_ge(S["w_max"], 5)
                    mm(m7[:, 3 * P:3 * P + 5], ones[:], wmax[:], start=True, stop=True).then_inc(S["w_sum"], 1)
                if c >= C - 3:
                    if c == C - 3:
                        pe.wait_ge(S["x_lo"], 1)
                        pe.wait_ge(S["adj_lo"], 1 + C // 2)
                    adj_x0(0, 2 * (c - C + 3), 2 * (c - C + 4))
            adj_x0(0, C - 2)
            pe.wait_ge(S["adj_lo"], C + 1)

            def body(i, nxt, cur, prev, last):
                t8 = i * C

                def scores(t):
                    if t == 0:
                        pe.wait_ge(S["v_lo"], 2 * (i + 1))
                    elif t == 1:
                        if last:
                            pe.wait_ge(S["fa"], i - 1)
                    else:
                        pe.wait_ge(S["th"], t8 + t - 1)
                    dst = (r1, r0)[t % 2]
                    for h in range(2):
                        l_ = split_product(dst[:, half(h)], x1T[:, 0, chunk(t)], x1T[:, 1, chunk(t)],
                                           gr[:, 0, half(h)], gr[:, 1, half(h)], True, True)
                    l_.then_inc(S["s_mm"], 1)

                def attend(t):
                    pe.wait_ge(S["pl"], t8 + t + 1)
                    if t == 0 and not is_first(i, 0):
                        pe.wait_ge(S["e1a"], i)
                    s = t % RING
                    for j in range(C):
                        o = (j % 3) * AVW
                        acc = av[:, j // 3, o:o + D + 1]
                        mm(acc, p_hi[:, s, chunk(j)], vhi[:, t, 0:D + 1], start=(t == 0 and j % 3 == 0), stop=False,
                           skip_group_check=True)
                        mm(acc[:, 0:D], p_hi[:, s, chunk(j)], vlo[:, t, :], start=False, stop=False, skip_group_check=True)
                        l_ = mm(acc, p_lo[:, s, chunk(j)], vhs[:, t, 0:D + 1], start=False, stop=(t == C - 1),
                                skip_group_check=True)
                    l_.then_inc(S["av_mm"], 1)

                def adj_x2(part):
                    h, m0 = part // 4, 2 * (part % 4)
                    if part == 0:
                        pe.wait_ge(S["l2_c"], L2_LINKS * (i - 1) + 1)
                    if part == 4:
                        pe.wait_ge(S["y2_lo"], 2 * i - 1)
                    for m in range(m0, m0 + 2):
                        l_ = split_product(m7[:], x2s[:, 0, m], x2s[:, 1, m], a_hi[:, m, half(h)], a_lo[:, m, half(h)],
                                           m == 0, m == C - 1)
                    if part % 4 == 3:
                        l_.then_inc(S["y2_mm"], 1)

                def sums():
                    pe.wait_ge(S["e1b"], i)
                    if last:
                        pe.wait_ge(S["y2_lo"], 2 * (i - 1))
                    for j in range(C):
                        mm(m7[:, 0:3], x2s[:, 0, j], one_sj[:, j], start=(j == 0), stop=False, skip_group_check=True)
                        l_ = mm(m7[:, 0:2], x2s[:, 1, j], one_sj[:, j, 0:2], start=False, stop=(j == C - 1),
                                skip_group_check=True)
                    l_.then_inc(S["xx_mm"], 1)

                late = is_first(i, 0) or is_first(i, 1)
                if cur:
                    scores(0)
                    scores(1)
                if late:
                    scores(2)
                if nxt and cur:
                    if last:
                        pe.wait_ge(S["y2_lo"], 2 * (i - 1))
                    pe.wait_ge(S["x_max"], i + 2)
                    mm(m7[:, 4:5], ones[:], xmax[:], start=True, stop=True).then_inc(S["x_sum"], 1)
                if prev:
                    sums()
                if cur and not late:
                    scores(2)
                if prev:
                    pe.wait_ge(S["xb_ok"], i)
                    if nxt and cur:
                        pe.wait_ge(S["x_st"], 5 * (i + 1) + 1)
                    mm(m7[:, 0:P], xb[:, 0], w2_sb[:], start=True, stop=True)
                    mm(m7[:, P:2 * P], xb[:, 1], w2_sb[:], start=True, stop=True).then_inc(S["rr_mm"], 1)
                for t in range(AHEAD, C):
                    if cur:
                        scores(t)
                    if prev and t == AHEAD:
                        adj_x2(0)
                        adj_x2(1)
                    if cur:
                        attend(t - AHEAD)
                    if prev and AHEAD < t < C - 2:
                        adj_x2(t - AHEAD + 1)
                if prev:
                    adj_x2(C - AHEAD - 1)
                for t in range(C - AHEAD, C):
                    if cur:
                        attend(t)
                    if prev and t == C - AHEAD:
                        for part in range(t, C):
                            adj_x2(part)
                if prev:
                    pe.wait_ge(S["y2_lo"], 2 * i)
                    if cur:
                        pe.wait_ge(S["th"], t8 + C)
                    elif last:
                        pe.wait_ge(S["fa"], i - 1)
                    project(r0, yT, w2s[:, 0], w2s[:, 1]).then_inc(S["p2_mm"], 1)
                if nxt:
                    if cur:
                        pe.wait_ge(S["th"], t8 + C - 1)
                        pe.wait_ge(S["x_lo"], i + 2)
                        adj_x0(0)
                    adj_x0(1, 0, C - 3)

                def layer0_half(h):
                    pe.wait_ge(S["y0_lo"], 2 * (i + 1) + h + 1)
                    project_half(r1, yT, w0s[:, 0], w0s[:, 1], h).then_inc(S["p0_mm"], 1)

                if nxt:
                    if is_first(i, -1):
                        adj_x0(1, C - 3)
                        pe.wait_ge(S["w_red"], 12)
                    layer0_half(0)
                    if not is_first(i, -1):
                        adj_x0(1, C - 3)
                if prev:
                    pe.wait_ge(S["ln2_v"], i)
                    transpose_half(r0, x3, 0).then_inc(S["x3t_mm"], 1)
                    pe.wait_ge(S["ln2_a"], i)
                    transpose_half(r0, x3, 1).then_inc(S["x3t_mm"], 1)
                if nxt:
                    layer0_half(1)
                if prev:
                    if cur:
                        pe.wait_ge(S["e1a"], i + 1)
                    for h in range(2):
                        pe.wait_ge(S["x3t_lo"], 2 * (i - 1) + h + 1)
                        project_half(r2, xq, w3s[:, 0, 0], w3s[:, 0, 1], h).then_inc(S["r_mm"], 1)
                    project(r0, xq, w3s[:, 1, 0], w3s[:, 1, 1]).then_inc(S["p_mm"], 1)
                    pe.wait_ge(S["r_lo"], 2 * i - 1)
                    project_half(r2, xq, w3s[:, 2, 0], w3s[:, 2, 1], 0)
                    pe.wait_ge(S["r_lo"], 2 * i)
                    project_half(r2, xq, w3s[:, 2, 0], w3s[:, 2, 1], 1).then_inc(S["u_mm"], 1)
                    pe.wait_ge(S["p_cp"], i)
                    if is_first(i, 1):
                        pe.wait_ge(S["lap_lo"], C)
                    apply_laplacian(r0, gr, 0, C // 2).then_inc(S["t_mm"], 1)
                    apply_laplacian(r0, gr, C // 2, C - 1)
                if is_first(i, -1):
                    pe.wait_ge(S["diag_ok"], 1)
                    for c in range(C):
                        l_ = mm(r0[:, chunk(c)], ones[:], tmp[:, c], start=True, stop=True)
                    l_.then_inc(S["dbc_mm"], 1)
                if nxt:
                    pe.wait_ge(S["ln0_v"], i + 2)
                    transpose_half(r1, x1, 0).then_inc(S["x1t_mm"], 1)
                    pe.wait_ge(S["ln0_a"], i + 2)
                    transpose_half(r1, x1, 1).then_inc(S["x1t_mm"], 1)
                if prev:
                    apply_laplacian(r0, gr, C - 1, C).then_inc(S["t_mm"], 1)
                if nxt:
                    if prev:
                        pe.wait_ge(S["u_ok"], i)
                    for h in range(2):
                        pe.wait_ge(S["x1t_lo"], 2 * (i + 1) + h + 1)
                        split_product(r2[:, half(h)], ms[:, 0], ms[:, 1], x1T[:, 0, half(h)], x1T[:, 1, half(h)],
                                      True, True).then_inc(S["g_mm"], 1)
                    for h in range(2):
                        project_half(r1, x1T, vs[:, 0], vs[:, 1], h).then_inc(S["v_mm"], 1)
                if prev:
                    pe.wait_ge(S["q_lo"], 2 * i)
                    apply_laplacian(r0, xq, 0, C).then_inc(S["o_mm"], 1)

            iterations(pe, body)


_INS = ["x", "adj", "L0_gnn_weight", "L0_gnn_bias", "L1_gnn_q", "L1_gnn_k", "L1_gnn_v", "L2_gnn_g_w", "L2_gnn_g_b",
        "L2_gnn_weight", "L2_gnn_bias", "L3_gnn_weight", "L3_gnn_bias"]


def kernel(**inputs):
    import numpy as _np
    import concourse.bacc as _bacc
    from concourse import mybir as _mybir
    from concourse.bass_utils import run_bass_kernel_spmd as _run

    nc = _bacc.Bacc("TRN2", target_bir_lowering=False, num_devices=1)
    arrays, args = {}, []
    for name in _INS:
        a = _np.ascontiguousarray(inputs[name])
        if a.ndim == 0:
            a = a.reshape(1)
        arrays[f"in_{name}"] = a
        args.append(nc.dram_tensor(f"in_{name}", a.shape, _mybir.dt.from_np(a.dtype), kind="ExternalInput").ap())
    args.append(nc.dram_tensor("out_0", (B, N, D), _mybir.dt.float32, kind="ExternalOutput").ap())
    adj_resnorm(nc, *args)
    r = _run(nc, [arrays], core_ids=[0])
    return r.results[0]["out_0"]
```

```python
import concourse.bass as bass
from concourse import mybir
from contextlib import ExitStack
import numpy as np

F32 = mybir.dt.float32
F16 = mybir.dt.float16
U32 = mybir.dt.uint32
ALU = mybir.AluOpType
ACT = mybir.ActivationFunctionType
AX = mybir.AxisListType

B, N, D = 8, 1024, 128
P = 128
C = N // P
HALF = 512
EPS = 1e-5
NORM_FLOOR = 1e-12
MIN_MAX = 1e-30
POW2_MASK = 0x7F800000

X_UP = 16.0
SUM_UP = 4096.0
SJ_UP = 1024.0
W_DOWN = 1.0 / 32
Q_DOWN = 1.0 / 4
ADJ_UP = 256.0
LAP_UP = 64.0
LO_UP = 2048.0
P_UP = 16.0
Y0_DOWN = 1.0 / 1024
Y2_DOWN = 1.0 / 1024
TANH_CAP = 8.0
ROOT, ARG, SHIFT = 5, 6, 7
LN_ARG = 5
LN_LINKS = 6
END_PARTS = ((0, 6), (6, 8))
END = 4
L2_LINKS = 4
V_CHUNKS = 5
AVW = 130
RING = 4
AHEAD = 3


class Count:

    def __init__(self, eng, sem, b, per):
        self.eng, self.sem, self.base, self.per, self.n = eng, sem, b * per, per, 0

    def mark(self, ins):
        ins.then_inc(self.sem, 1)
        self.n += 1

    def wait(self):
        self.eng.wait_ge(self.sem, self.base + self.n)

    def link(self, ins):
        self.mark(ins)
        self.wait()

    def end(self):
        assert self.n == self.per, (self.n, self.per)


class Stage:

    def __init__(self, x3, xq, gr, pq, u, outb, acc):
        self.x3, self.xq, self.gr, self.pq, self.u, self.outb, self.acc = x3, xq, gr, pq, u, outb, acc


def adj_resnorm(nc, x, adj, w0, b0, q, k, v, gw, gb, w2, b2, w3, b3, out):
    ctx = ExitStack()
    with ctx:
        def sb(name, shape, dt=F32):
            return ctx.enter_context(nc.sbuf_tensor(name, shape, dt))

        def ps(name, shape):
            return ctx.enter_context(nc.psum_tensor(name, shape, F32))

        def sem(name):
            return ctx.enter_context(nc.semaphore(name))

        adjT = sb("adjT", [P, C, N])
        a_hi = sb("a_hi", [P, C, N], F16)
        a_lo = sb("a_lo", [P, C, N], F16)
        lap = sb("lap", [P, 2, C, N], F16)
        adj_rows = lap[:].rearrange("p a c n -> p (a c n)").bitcast(F32).rearrange("p (c n) -> p c n", c=C)
        ident = sb("ident", [P, P])
        ident_up = sb("ident_up", [P, P], F16)
        ones = sb("ones", [P, P])
        w2_sb = sb("w2_sb", [P, D])
        w0s, ms, vs, w2s = (sb(n_, [P, 2, D], F16) for n_ in ("w0s", "ms", "vs", "w2s"))
        w3s = sb("w3s", [P, 3, 2, D], F16)
        wjp = sb("wjp", [P, 4])
        b0_bc, b2_bc, b3_bc, wj_bc, wi_bc = (sb(n_, [P, D]) for n_ in ("b0_bc", "b2_bc", "b3_bc", "wj_bc", "wi_bc"))
        wr_gb = sb("wr_gb", [P, 2])
        wmax, wpow, winv = (sb(n_, [P, 5]) for n_ in ("wmax", "wpow", "winv"))
        coef = sb("coef", [P, 8])
        c_w0, c_tanh, c_v, c_l2, c_u, c_o = (coef[:, j:j + 1] for j in range(6))
        deg, dis = sb("deg", [P, C]), sb("dis", [P, C])
        x0 = sb("x0", [P, C, D])
        xmax, xpow, xinv, c_y0 = (sb(n_, [P, 1]) for n_ in ("xmax", "xpow", "xinv", "c_y0"))
        x0s = sb("x0s", [P, 2, C, D], F16)
        yT = sb("yT", [P, 2, N], F16)
        x1 = sb("x1", [P, C, D])
        x1T = sb("x1T", [P, 2, N], F16)
        gr = sb("gr", [P, 2, N], F16)
        vhi = sb("vhi", [P, C, AVW], F16)
        vlo = sb("vlo", [P, C, D], F16)
        vhs = sb("vhs", [P, C, AVW], F16)
        att = sb("att", [P, RING, N])
        p_hi, p_lo = sb("p_hi", [P, RING, N], F16), sb("p_lo", [P, RING, N], F16)
        x2 = sb("x2", [P, C, D])
        w0_sb, q_sb, k_sb, v_sb, qT, kT, m_sb = (x2[:, j] for j in range(7))
        x2s = sb("x2s", [P, 2, C, D], F16)
        one_sj = sb("one_sj", [P, C, 3], F16)
        sj = sb("sj", [P, C])
        sig = sb("sig", [P, C])
        tmp = sb("tmp", [P, C, D])
        xs = sb("xs", [P, 4])
        xb = sb("xb", [P, 2, P])
        r2b = sb("r2b", [P, D])
        x3 = sb("x3", [P, C, D])
        w3_sb, w3c = x3[:, 0:3], x3[:, 3:6]
        xq = sb("xq", [P, 2, N], F16)
        pq = sb("pq", [P, C, D])
        u = sb("u", [P, C, D])
        outb = sb("outb", [P, C, D])
        stats = sb("stats", [P, 5, C, 2, 3])
        pair = sb("pair", [P, C, 2])
        minus_half = sb("minus_half", [P, C])
        small = sb("small", [P, 5, 8, C])
        rsum, rinv = sb("rsum", [P, 9]), sb("rinv", [P, C])
        junk = att[:].rearrange("p r n -> p (r n)").bitcast(F16)
        dis_bc = pq[:].rearrange("p c d -> p (c d)")
        lap_f = u[:].rearrange("p c d -> p (c d)")
        lap_g = outb[:].rearrange("p c d -> p (c d)")

        r0 = ps("r0", [P, N])
        r1 = ps("r1", [P, N])
        av = ps("av", [P, 3, HALF])
        m7 = ps("m7", [P, HALF])
        r2 = av[:].rearrange("p a n -> p (a n)")[:, 0:N]

        def cd(ap):
            return ap.rearrange("p (c d) -> p c d", c=C)

        z_all = Stage(x3, xq, gr, pq, u, outb, r0)
        z_end = Stage(cd(att[:, 0]), x1T, p_hi[:, 0:2], cd(att[:, 1]), cd(att[:, 2]), cd(att[:, 3]), r1)

        names = ("w_in wq_in x_in ident_ok const_ok qk_t qk_c m_cp m_mm w_max w_sum w_red w_ok wj_c "
                 "tr adj_hi adj_cp adj_lo deg_ok diag_ok dbc_mm lap_st lap_hi lap_lo "
                 "norm_r dis_ok x_max x_sum x_st x_hi x_lo "
                 "y0_mm y0_hi y0_lo p0_mm e0_c e0 x1t_mm x1t_hi x1t_lo g_mm g_hi g_lo v_mm v_hi v_s v_lo "
                 "s_mm th ex pm ph pl av_mm e1a e1a_c x2_hi sj_c e1b "
                 "xx_mm xb_c xb_ok y2_mm y2_hi y2_lo rr_mm p2_mm l2_c x3t_mm x3t_hi x3t_lo "
                 "r_mm r_hi r_lo p_mm p_cp u_mm u_ok t_mm q_ok q_hi q_lo o_mm fa f_c stored").split()
        names += [f"ln{k_}{end}" for k_ in range(4) for end in ("", "_r", "_v", "_a")]
        S = {n_: sem(n_) for n_ in names}
        adj_in = [sem(f"adj_in{c}") for c in range(C)]

        block = ctx.enter_context(nc.Block())

        def half(h):
            return slice(h * HALF, (h + 1) * HALF)

        def chunk(c):
            return slice(c * P, (c + 1) * P)

        def half_chunks(h):
            return slice(h * C // 2, (h + 1) * C // 2)

        def is_first(i, n):
            return isinstance(i, int) and i == n

        def iterations(eng, body):
            body(-1, True, False, False, False)
            body(0, True, True, False, False)
            body(1, True, True, True, False)
            body(2, True, True, True, True)
            with eng.Fori(3, B - 1) as i:
                body(i, True, True, True, True)
            body(B - 1, False, True, True, True)

        x_v = x.rearrange("b (c p) d -> b p c d", p=P)

        @block.sync
        def _(sp):
            sp.dma_start(x0[:], x_v[0]).then_inc(S["x_in"], 16)
            adj_v = adj.rearrange("(c p) m -> c p m", p=P)
            for c in range(C):
                sp.dma_start(adj_rows[:, c, :], adj_v[c]).then_inc(adj_in[c], 16)
                if c == 1:
                    for dst, src in ((b0_bc[:], b0), (b2_bc[:], b2), (b3_bc[:], b3.rearrange("a b d -> (a b d)")),
                                     (wj_bc[:], gw[0:D]), (wi_bc[:], gw[D:2 * D]),
                                     (wr_gb[:, 0:1], gw[2 * D:2 * D + 1]), (wr_gb[:, 1:2], gb)):
                        sp.dma_start(dst, src.partition_broadcast(P)).then_inc(S["w_in"], 16)
            out_v = out.rearrange("b (c p) d -> b p c d", p=P)

            def body(i, nxt, cur, prev, last):
                if nxt and cur:
                    sp.wait_ge(S["e0"], i + 1)
                    sp.dma_start(x0[:], x_v[i + 1]).then_inc(S["x_in"], 16)
                if last:
                    sp.wait_ge(S["ln3_a"], i - 1)
                    sp.dma_start(out_v[i - 2], outb[:]).then_inc(S["stored"], 16)

            iterations(sp, body)
            sp.wait_ge(S["ln3_a"], B - 1)
            sp.dma_start(out_v[B - 2], outb[:]).then_inc(S["stored"], 16)
            for h, (first, end) in enumerate(END_PARTS):
                sp.wait_ge(S["ln3_v"], h + 1)
                sp.wait_ge(S["ln3_a"], B + h)
                sp.dma_start(out_v[B - 1][:, first:end], z_end.outb[:, first:end]).then_inc(S["stored"], 16)
            sp.wait_ge(S["stored"], 16 * (B + 1))

        @block.gpsimd
        def _(pool):
            nc.gpsimd.memset(ident[:], 0.0).then_inc(S["ident_ok"], 1)
            pool.wait_ge(S["ident_ok"], 1)
            nc.gpsimd.affine_select(out=ident[:], in_=ident[:], compare_op=ALU.not_equal, fill=1.0, base=0,
                                    pattern=[[-1, P]], channel_multiplier=1).then_inc(S["ident_ok"], 1)
            nc.gpsimd.memset(minus_half[:], -0.5).then_inc(S["ident_ok"], 1)
            pool.wait_ge(S["ident_ok"], 3)

            def inverse_root(dst, src):
                return nc.gpsimd.tensor_tensor(dst, src, minus_half[:], ALU.pow)

            def norm_root(k_, b):
                pool.wait_ge(S[f"ln{k_}"], LN_LINKS * b + LN_ARG)
                inverse_root(small[:, k_, ROOT], small[:, k_, ARG]).then_inc(S[f"ln{k_}_r"], 1)

            def body(i, nxt, cur, prev, last):
                if is_first(i, B - 1):
                    return
                if prev:
                    norm_root(2, i - 1)
                if last:
                    norm_root(3, i - 2)
                if is_first(i, -1):
                    pool.wait_ge(S["deg_ok"], C)
                    inverse_root(dis[:], deg[:]).then_inc(S["dis_ok"], 1)
                if nxt:
                    pool.wait_ge(S["e0_c"], 8 * (i + 2))
                    inverse_root(small[:, 4, ROOT], small[:, 4, ARG]).then_inc(S["norm_r"], 1)
                if nxt:
                    norm_root(0, i + 1)
                if cur:
                    norm_root(1, i)

            iterations(pool, body)
            norm_root(2, B - 2)
            norm_root(3, B - 3)
            norm_root(1, B - 1)
            norm_root(2, B - 1)
            norm_root(3, B - 2)
            for h, part in enumerate(END_PARTS):
                hc = slice(*part)
                pool.wait_ge(S["ln3"], LN_LINKS * (B - 1) + LN_ARG * (h + 1))
                nc.gpsimd.tensor_tensor(small[:, END, ROOT, hc], small[:, END, ARG, hc], minus_half[:, hc],
                                        ALU.pow).then_inc(S["ln3_r"], 1)

        @block.scalar
        def _(act):
            for dst, src in ((q_sb, q), (k_sb, k)):
                act.dma_start(dst, src).then_inc(S["wq_in"], 16)
            for dst, src in ((w0_sb, w0), (v_sb, v), (w2_sb[:], w2)):
                act.dma_start(dst, src).then_inc(S["w_in"], 16)
            act.dma_start(w3_sb, w3.rearrange("k o c d -> c (k o) d")).then_inc(S["w_in"], 16)

            def copy(dst, src, scale=1.0, **more):
                return nc.scalar.activation(dst, src, ACT.Copy, scale=scale, **more)

            def x0_hi(b):
                act.wait_ge(S["x_st"], 5 * (b + 1))
                copy(x0s[:, 0], x0[:], xinv[:]).then_inc(S["x_hi"], 1)

            x0_hi(0)
            for c in range(C):
                act.wait_ge(S["tr"], c + 1)
                src = cd((r0[:], r2)[c % 2])
                copy(a_hi[:, :, chunk(c)], src, ADJ_UP).then_inc(S["adj_hi"], 1)
                copy(adjT[:, :, chunk(c)], src, LO_UP * P_UP).then_inc(S["adj_cp"], 1)

            def degrees(first, last_):
                for c in range(first, last_):
                    copy(junk[:, c * N:(c + 1) * N], adj_rows[:, c, :], accum_out=deg[:, c:c + 1]).then_inc(S["deg_ok"], 1)

            def lap_hi_part(*rows):
                for c in rows:
                    act.wait_ge(S["lap_st"], 2 * (c + 1))
                    copy(lap[:, 0, c, :], (lap_f, lap_g)[c % 2]).then_inc(S["lap_hi"], 1)

            def norm(k_, b, t, first):
                act.wait_ge(S[f"ln{k_}"], LN_LINKS * (b + 1))
                for j in range(first, C):
                    l_ = nc.scalar.activation(t[:, j], t[:, j], ACT.Identity, scale=small[:, k_, ROOT, j:j + 1],
                                              bias=small[:, k_, SHIFT, j:j + 1])
                l_.then_inc(S[f"ln{k_}_a"], 1)

            def copy_x2(b):
                act.wait_ge(S["ln1_v"], b + 1)
                act.wait_ge(S["ln1_a"], b + 1)
                if not is_first(b, 0):
                    act.wait_ge(S["y2_mm"], 2 * b)
                copy(x2s[:, 0], x2[:], X_UP).then_inc(S["x2_hi"], 1)

            def y2_hi(b, h):
                act.wait_ge(S["y2_mm"], 2 * b + h + 1)
                copy(yT[:, 0, half(h)], m7[:], Y2_DOWN).then_inc(S["y2_hi"], 1)

            def x3t_hi(z, b, h):
                act.wait_ge(S["x3t_mm"], 2 * b + h + 1)
                copy(z.xq[:, 0, half(h)], z.acc[:, half(h)], X_UP).then_inc(S["x3t_hi"], 1)

            def r_hi(z, b, h):
                act.wait_ge(S["r_mm"], 2 * b + h + 1)
                copy(z.gr[:, 0, half(h)], r2[:, half(h)], W_DOWN).then_inc(S["r_hi"], 1)

            def p_copy(z, b):
                act.wait_ge(S["p_mm"], b + 1)
                copy(z.pq[:], cd(z.acc[:]), W_DOWN * Q_DOWN).then_inc(S["p_cp"], 1)

            def q_hi(z, b, h):
                act.wait_ge(S["q_ok"], 2 * b + h + 1)
                if h == 0:
                    act.wait_ge(S["u_mm"], b + 1)
                copy(cd(z.xq[:, 0])[:, half_chunks(h)], z.pq[:, half_chunks(h)]).then_inc(S["q_hi"], 1)

            def body(i, nxt, cur, prev, last):
                t8 = i * C

                def y2_half(h):
                    if h == 0:
                        act.wait_ge(S["p0_mm"], 2 * (i + 1))
                    y2_hi(i - 1, h)

                def y0_half(h):
                    act.wait_ge(S["y0_mm"], 2 * (i + 1) + h + 1)
                    if prev and h == 0:
                        act.wait_ge(S["p2_mm"], i)
                    copy(yT[:, 0, half(h)], m7[:] if is_first(i, 0) else r1[:, half(h)], Y0_DOWN).then_inc(S["y0_hi"], 1)

                def p_hi_part(t):
                    act.wait_ge(S["pm"], t8 + t + 1)
                    if not (is_first(i, 0) and t < RING):
                        act.wait_ge(S["av_mm"], t8 + t - RING + 1)
                    s = t % RING
                    copy(p_hi[:, s], att[:, s], 1.0 / LO_UP).then_inc(S["ph"], 1)

                if cur:
                    for t in range(C):
                        s = t % RING
                        act.wait_ge(S["s_mm"], t8 + t + 1)
                        if not (is_first(i, 0) and t < RING):
                            act.wait_ge(S["pl"], t8 + t - RING + 1)
                        nc.scalar.activation(att[:, s], (r1, r0)[t % 2][:], ACT.Tanh, scale=c_tanh).then_inc(S["th"], 1)
                        act.wait_ge(S["th"], t8 + t + 1)
                        nc.scalar.activation(att[:, s], att[:, s], ACT.Exp, scale=TANH_CAP).then_inc(S["ex"], 1)
                        if t >= 1:
                            p_hi_part(t - 1)
                        if t == 5 and prev:
                            y2_half(0)
                        if is_first(i, 1) and t in (2, 4, 7):
                            lap_hi_part({2: 5, 4: 6, 7: 7}[t])
                        if is_first(i, 0):
                            if t == 1:
                                act.wait_ge(S["y0_mm"], 2)
                                x0_hi(1)
                            if t == 2:
                                lap_hi_part(2)
                            if t == 5:
                                lap_hi_part(3)
                    if is_first(i, 0):
                        y0_half(0)
                    p_hi_part(C - 1)
                    if is_first(i, 0):
                        lap_hi_part(4)
                if is_first(i, B - 1):
                    return
                if nxt and prev:
                    act.wait_ge(S["y0_mm"], 2 * (i + 1))
                    x0_hi(i + 1)
                if prev:
                    y2_half(1)
                if nxt and not is_first(i, 0):
                    y0_half(0)
                if prev:
                    norm(2, i - 1, x3, V_CHUNKS)
                if is_first(i, -1):
                    degrees(0, 5)
                if nxt:
                    y0_half(1)
                if is_first(i, -1):
                    degrees(5, C)
                if prev:
                    if last:
                        act.wait_ge(S["o_mm"], 2 * (i - 1))
                    for h in range(2):
                        x3t_hi(z_all, i - 1, h)
                    for h in range(2):
                        r_hi(z_all, i - 1, h)
                    if last:
                        act.wait_ge(S["q_lo"], 2 * (i - 1))
                    if is_first(i, 1):
                        act.wait_ge(S["lap_st"], 2 * C)
                    p_copy(z_all, i - 1)
                if last:
                    norm(3, i - 2, outb, 0)
                if prev:
                    q_hi(z_all, i - 1, 0)
                if nxt:
                    norm(0, i + 1, x1, V_CHUNKS)
                    for h in range(2):
                        act.wait_ge(S["x1t_mm"], 2 * (i + 1) + h + 1)
                        copy(x1T[:, 0, half(h)], r1[:, half(h)], X_UP).then_inc(S["x1t_hi"], 1)
                if is_first(i, -1):
                    lap_hi_part(0)
                if prev:
                    q_hi(z_all, i - 1, 1)
                if cur:
                    norm(1, i, x2, V_CHUNKS)
                if nxt:
                    for h in range(2):
                        act.wait_ge(S["g_mm"], 2 * (i + 1) + h + 1)
                        if prev and h == 0:
                            act.wait_ge(S["t_mm"], 2 * i)
                        copy(gr[:, 0, half(h)], r2[:, half(h)], W_DOWN).then_inc(S["g_hi"], 1)
                    for h in range(2):
                        act.wait_ge(S["v_mm"], 2 * (i + 1) + h + 1)
                        if cur and h == 0:
                            act.wait_ge(S["av_mm"], C * (i + 1))
                        copy(vhi[:, half_chunks(h), 0:D], cd(r1[:])[:, half_chunks(h)], W_DOWN).then_inc(S["v_hi"], 1)
                    act.wait_ge(S["v_hi"], 2 * (i + 2))
                    copy(vhs[:, :, 0:D], vhi[:, :, 0:D], 1.0 / LO_UP).then_inc(S["v_s"], 1)
                if is_first(i, -1):
                    lap_hi_part(1)
                if cur:
                    copy_x2(i)

            iterations(act, body)
            y2_hi(B - 2, 1)
            norm(2, B - 2, x3, V_CHUNKS)
            act.wait_ge(S["o_mm"], 2 * (B - 2))
            for h in range(2):
                x3t_hi(z_all, B - 2, h)
            norm(1, B - 1, x2, V_CHUNKS)
            copy_x2(B - 1)
            for h in range(2):
                r_hi(z_all, B - 2, h)
            act.wait_ge(S["q_lo"], 2 * (B - 2))
            p_copy(z_all, B - 2)
            norm(3, B - 3, outb, 0)
            act.wait_ge(S["p2_mm"], B - 1)
            for h in range(2):
                y2_hi(B - 1, h)
            q_hi(z_all, B - 2, 0)
            norm(2, B - 1, z_end.x3, V_CHUNKS)
            for h in range(2):
                x3t_hi(z_end, B - 1, h)
            q_hi(z_all, B - 2, 1)
            for h in range(2):
                r_hi(z_end, B - 1, h)
            p_copy(z_end, B - 1)
            for h in range(2):
                q_hi(z_end, B - 1, h)
            norm(3, B - 2, outb, 0)
            for h, (first, end) in enumerate(END_PARTS):
                act.wait_ge(S["ln3"], LN_LINKS * (B - 1) + 2 * LN_ARG + 1 + h)
                for j in range((first + end) // 2, end):
                    l_ = nc.scalar.activation(z_end.outb[:, j], z_end.outb[:, j], ACT.Identity,
                                              scale=small[:, END, ROOT, j:j + 1], bias=small[:, END, SHIFT, j:j + 1])
                l_.then_inc(S["ln3_a"], 1)

        @block.vector
        def _(dve):
            tt = nc.vector.tensor_tensor
            ts = nc.vector.tensor_scalar
            stt = nc.vector.scalar_tensor_tensor

            def row(ap, n=C):
                return ap.unsqueeze(1).to_broadcast([P, n, D])

            def chunk_stats(k_, src, chunks=range(C)):
                for j in chunks:
                    l_ = nc.vector.bn_stats(stats[:, k_, j].rearrange("p a k -> p (a k)"), src[:, j])
                return l_

            def ln_stats(k_, b, src):
                chunk_stats(k_, src).then_inc(S[f"ln{k_}"], 1)

            def ln_arg(k_, b, cs=slice(0, C), at=None, before=0):
                ch = Count(dve, S[f"ln{k_}"], b, LN_ARG)
                ch.base, ch.n = LN_LINKS * b + before, 1
                ch.wait()
                at = k_ if at is None else at
                st, sm = stats[:, at, cs], small[:, at, :, cs]
                me, mo = st[:, :, 0, 1], st[:, :, 1, 1]
                tt(sm[:, 0], me, mo, ALU.add)
                tt(sm[:, 1], me, mo, ALU.subtract)
                ch.link(tt(sm[:, 2], st[:, :, 0, 2], st[:, :, 1, 2], ALU.add))
                tt(sm[:, 3], sm[:, 1], sm[:, 1], ALU.mult)
                ch.link(ts(sm[:, 4], sm[:, 0], -0.5, None, ALU.mult))
                ch.link(stt(sm[:, 0], sm[:, 3], D / 4.0, sm[:, 2], ALU.mult, ALU.add))
                ch.mark(ts(sm[:, ARG], sm[:, 0], 1.0 / D, EPS, ALU.mult, ALU.add))
                ch.end()

            def ln_begin(k_, b, src):
                ln_stats(k_, b, src)
                ln_arg(k_, b)

            def ln_shift(k_, b):
                dve.wait_ge(S[f"ln{k_}_r"], b + 1)
                sm = small[:, k_]
                tt(sm[:, SHIFT], sm[:, 4], sm[:, ROOT], ALU.mult).then_inc(S[f"ln{k_}"], 1)

            def ln_norm(k_, b, t):
                dve.wait_ge(S[f"ln{k_}"], LN_LINKS * (b + 1))
                sm = small[:, k_]
                for j in range(V_CHUNKS):
                    l_ = ts(t[:, j], t[:, j], sm[:, ROOT, j:j + 1], sm[:, SHIFT, j:j + 1], ALU.mult, ALU.add)
                l_.then_inc(S[f"ln{k_}_v"], 1)

            nc.vector.memset(ones[:], 1.0)
            nc.vector.memset(one_sj[:, :, 0:1], 1.0)
            nc.vector.memset(vhi[:, :, D:D + 1], 1.0)
            nc.vector.memset(vhs[:, :, D:D + 1], 1.0 / LO_UP).then_inc(S["const_ok"], 1)

            def x0_max(b):
                dve.wait_ge(S["x_in"], 16 * (b + 1))
                nc.vector.tensor_reduce(xmax[:], x0[:].rearrange("p c d -> p (c d)"), AX.X, ALU.max,
                                        apply_absolute_value=True).then_inc(S["x_max"], 1)

            def x0_scale_read(b):
                dve.wait_ge(S["x_sum"], b + 1)
                ts(xpow[:], m7[:, 4:5], MIN_MAX, None, ALU.max).then_inc(S["x_st"], 1)

            def x0_scales(b):
                ch = Count(dve, S["x_st"], b, 5)
                ch.n = 1
                ch.wait()
                ch.link(ts(xpow[:].bitcast(U32), xpow[:].bitcast(U32), POW2_MASK, None, ALU.bitwise_and))
                ch.link(nc.vector.reciprocal(xinv[:], xpow[:]))
                ch.mark(ts(c_y0[:], xpow[:], 1.0 / SUM_UP, None, ALU.mult))
                ch.mark(ts(xinv[:], xinv[:], SUM_UP, None, ALU.mult))
                ch.end()

            def x0_lo(b):
                dve.wait_ge(S["x_hi"], b + 1)
                stt(x0s[:, 1], x0[:], xinv[:], x0s[:, 0], ALU.mult, ALU.subtract).then_inc(S["x_lo"], 1)

            x0_max(0)
            x0_scale_read(0)
            x0_scales(0)
            dve.wait_ge(S["qk_t"], 1)
            nc.vector.tensor_copy(qT, m7[:, 0:P])
            nc.vector.tensor_copy(kT, m7[:, P:2 * P]).then_inc(S["qk_c"], 1)
            x0_lo(0)
            dve.wait_ge(S["m_mm"], 1)
            nc.vector.tensor_copy(m_sb, m7[:, 2 * P:3 * P]).then_inc(S["m_cp"], 1)

            def weights_max():
                dve.wait_ge(S["w_in"], 16 * 11)
                tt(w3c[:, 2], w3_sb[:, 0], w3_sb[:, 2], ALU.subtract)
                nc.vector.tensor_copy(w3c[:, 0], w3_sb[:, 2])
                nc.vector.tensor_copy(w3c[:, 1], w3_sb[:, 1]).then_inc(S["m_cp"], 1)
                dve.wait_ge(S["m_cp"], 2)
                for j, w in enumerate((w0_sb, m_sb, v_sb, w2_sb[:], w3c.rearrange("p k d -> p (k d)"))):
                    nc.vector.tensor_reduce(wmax[:, j:j + 1], w, AX.X, ALU.max,
                                            apply_absolute_value=True).then_inc(S["w_max"], 1)

            def weights():
                ch = Count(dve, S["wj_c"], 0, 6)
                ch.link(nc.vector.tensor_reduce(wjp[:, 0:1], wj_bc[:], AX.X, ALU.add, apply_absolute_value=True))
                ch.link(ts(wjp[:, 1:2], wjp[:, 0:1], MIN_MAX, None, ALU.max))
                ch.link(ts(wjp[:, 1:2].bitcast(U32), wjp[:, 1:2].bitcast(U32), POW2_MASK, None, ALU.bitwise_and))
                ts(wjp[:, 3:4], wjp[:, 1:2], 1.0 / (X_UP * SJ_UP), None, ALU.mult)
                ch.link(nc.vector.reciprocal(wjp[:, 2:3], wjp[:, 1:2]))
                ch.link(ts(wjp[:, 2:3], wjp[:, 2:3], SJ_UP, None, ALU.mult))
                ch.link(ts(wj_bc[:], wj_bc[:], wjp[:, 2:3], None, ALU.mult))
                ch.end()
                dve.wait_ge(S["w_sum"], 1)
                ch = Count(dve, S["w_red"], 0, 12)
                ch.link(ts(wpow[:], m7[:, 3 * P:3 * P + 5], MIN_MAX, None, ALU.max))
                ch.link(ts(wpow[:].bitcast(U32), wpow[:].bitcast(U32), POW2_MASK, None, ALU.bitwise_and))
                ch.link(nc.vector.reciprocal(winv[:], wpow[:]))
                ch.link(ts(winv[:], winv[:], SUM_UP, None, ALU.mult))
                parts = ((w0_sb, w0s[:, 0], w0s[:, 1]), (m_sb, ms[:, 0], ms[:, 1]),
                         (v_sb, vs[:, 0], vs[:, 1]), (w2_sb[:], w2s[:, 0], w2s[:, 1]),
                         (w3c, w3s[:, :, 0], w3s[:, :, 1]))
                for j, (w, hi, lo) in enumerate(parts):
                    ch.link(ts(hi, w, winv[:, j:j + 1], None, ALU.mult))
                    l_ = stt(lo, w, winv[:, j:j + 1], hi, ALU.mult, ALU.subtract)
                ch.mark(l_)
                xw = X_UP * SUM_UP
                ts(c_w0, wpow[:, 0:1], 1.0 / (ADJ_UP * Y0_DOWN * SUM_UP), None, ALU.mult)
                ts(c_tanh, wpow[:, 1:2], 1.0 / (X_UP * xw * W_DOWN * float(np.sqrt(float(D))) * TANH_CAP), None, ALU.mult)
                ts(c_v, wpow[:, 2:3], 1.0 / (xw * W_DOWN), None, ALU.mult)
                ts(c_u, wpow[:, 4:5], 1.0 / xw, None, ALU.mult)
                ts(c_o, wpow[:, 4:5], 1.0 / (xw * W_DOWN * Q_DOWN * LAP_UP), None, ALU.mult)
                ch.link(ts(c_l2, wpow[:, 3:4], 1.0 / (xw * ADJ_UP * Y2_DOWN), None, ALU.mult))
                ch.link(ts(c_l2, c_l2, wr_gb[:, 0:1], None, ALU.mult))
                ch.end()

            for c in range(C):
                dve.wait_ge(S["adj_cp"], c + 1)
                stt(a_lo[:, :, chunk(c)], adjT[:, :, chunk(c)], ADJ_UP / (LO_UP * P_UP), a_hi[:, :, chunk(c)],
                    ALU.mult, ALU.subtract).then_inc(S["adj_lo"], 1)
                if c == C // 2:
                    weights_max()
                if c == 0:
                    dve.wait_ge(S["ident_ok"], 3)
                    ts(ident_up[:], ident[:], ADJ_UP, None, ALU.mult).then_inc(S["adj_lo"], 1)
            weights()

            def lap_row(*rows):
                for c in rows:
                    f = (lap_f, lap_g)[c % 2]
                    if c >= 2:
                        dve.wait_ge(S["lap_lo"], c - 1)
                    stt(f, adjT[:, c, :], dis[:, c:c + 1], dis_bc, ALU.mult, ALU.mult).then_inc(S["lap_st"], 1)
                    dve.wait_ge(S["lap_st"], 2 * c + 1)
                    stt(f[:, chunk(c)], ident[:], LAP_UP, f[:, chunk(c)], ALU.mult, ALU.add).then_inc(S["lap_st"], 1)

            def lap_lo_part(*rows):
                for c in rows:
                    dve.wait_ge(S["lap_hi"], c + 1)
                    tt(lap[:, 1, c, :], (lap_f, lap_g)[c % 2], lap[:, 0, c, :], ALU.subtract).then_inc(S["lap_lo"], 1)

            def split_lo(dst, src, scale, hi, name, count):
                dve.wait_ge(S[name + "_hi"], count)
                stt(dst, src, scale, hi, ALU.mult, ALU.subtract).then_inc(S[name + "_lo"], 1)

            def y2_lo(b, h):
                split_lo(yT[:, 1, half(h)], m7[:], Y2_DOWN, yT[:, 0, half(h)], "y2", 2 * b + h + 1)

            def sums_read(b, src):
                dve.wait_ge(S["xx_mm"], b + 1)
                nc.vector.tensor_copy(xs[:, 0:3], src[:, 0:3]).then_inc(S["xb_c"], 1)

            def sums(b):
                ch = Count(dve, S["xb_c"], b, 2)
                ch.n = 1
                ch.wait()
                ts(xb[:, 0], xs[:, 0:1].to_broadcast([P, P]), 1.0 / X_UP, None, ALU.mult)
                ch.link(tt(xs[:, 3:4], xs[:, 1:2], xs[:, 2:3], ALU.add))
                ch.end()
                ts(xb[:, 1], xs[:, 3:4].to_broadcast([P, P]), wjp[:, 3:4], None, ALU.mult).then_inc(S["xb_ok"], 1)

            def l2_read(ch, b, src):
                dve.wait_ge(S["rr_mm"], b + 1)
                nc.vector.tensor_copy(tmp[:, 0], src[:, 0:P])
                ch.mark(tt(r2b[:], src[:, P:2 * P], b2_bc[:], ALU.add))

            def l2_rank_one(ch, z):
                ch.wait()
                for j in range(C):
                    l_ = stt(z.x3[:, j], tmp[:, 0], sig[:, j:j + 1], x2[:, j], ALU.mult, ALU.add)
                ch.mark(l_)

            def l2_row(ch, z):
                ch.wait()
                ch.link(tt(z.x3[:], z.x3[:], row(r2b[:]), ALU.add))

            def l2_end(ch, z, b):
                dve.wait_ge(S["p2_mm"], b + 1)
                ch.link(stt(z.x3[:], cd(z.acc[:]), c_l2, z.x3[:], ALU.mult, ALU.add))
                ch.end()

            def x3t_lo(z, b, h):
                split_lo(z.xq[:, 1, half(h)], z.acc[:, half(h)], X_UP, z.xq[:, 0, half(h)], "x3t", 2 * b + h + 1)

            def r_lo(z, b, h):
                split_lo(z.gr[:, 1, half(h)], r2[:, half(h)], W_DOWN, z.gr[:, 0, half(h)], "r", 2 * b + h + 1)

            def u_part(z, b):
                dve.wait_ge(S["u_mm"], b + 1)
                stt(z.u[:], cd(r2), c_u, row(b3_bc[:]), ALU.mult, ALU.add).then_inc(S["u_ok"], 1)

            def q_part(z, b, h):
                hc = half_chunks(h)
                dve.wait_ge(S["t_mm"], 2 * b + h + 1)
                dve.wait_ge(S["p_cp"], b + 1)
                stt(z.pq[:, hc], cd(z.acc[:])[:, hc], 2.0 * Q_DOWN / LAP_UP, z.pq[:, hc],
                    ALU.mult, ALU.add).then_inc(S["q_ok"], 1)

            def q_lo(z, b, h):
                hc = half_chunks(h)
                dve.wait_ge(S["q_hi"], 2 * b + h + 1)
                tt(cd(z.xq[:, 1])[:, hc], z.pq[:, hc], cd(z.xq[:, 0])[:, hc], ALU.subtract).then_inc(S["q_lo"], 1)

            def end_sum(b, h):
                hc = half_chunks(h)
                dve.wait_ge(S["o_mm"], 2 * b + h + 1)
                stt(u[:, hc], cd(r0[:])[:, hc], c_o, u[:, hc], ALU.mult, ALU.add).then_inc(S["fa"], 1)

            def row_sums(b):
                ch = Count(dve, S["e1a_c"], b, 2)
                dve.wait_ge(S["av_mm"], C * (b + 1))
                for k_ in range(3):
                    w = min(3, C - 3 * k_)
                    l_ = nc.vector.reciprocal(rsum[:, 3 * k_:3 * k_ + w], av[:, k_, D:D + AVW * (w - 1) + 1:AVW])
                ch.link(l_)
                ch.link(ts(rinv[:], rsum[:, 0:C], c_v, None, ALU.mult))
                ch.end()

            def attention_residual(j):
                o = (j % 3) * AVW
                return stt(x2[:, j], av[:, j // 3, o:o + D], rinv[:, j:j + 1], x1[:, j], ALU.mult, ALU.add)

            def sj_step(ch, b, step):
                if step == 0:
                    dve.wait_ge(S["ln1_a"], b + 1)
                    dve.wait_ge(S["ln1_v"], b + 1)
                    ch.link(tt(tmp[:], x2[:], row(wj_bc[:]), ALU.mult))
                if step == 1:
                    ch.link(nc.vector.tensor_reduce(sj[:], tmp[:], AX.X, ALU.add))
                    nc.vector.tensor_copy(one_sj[:, :, 1], sj[:])
                if step == 2:
                    ch.link(tt(tmp[:], x2[:], row(wi_bc[:]), ALU.mult))
                    tt(one_sj[:, :, 2], sj[:], one_sj[:, :, 1], ALU.subtract)
                if step == 3:
                    ch.link(nc.vector.tensor_reduce(sig[:], tmp[:], AX.X, ALU.add))
                    ch.link(ts(sig[:], sig[:], wr_gb[:, 1:2], None, ALU.add))
                    ch.end()

            def x2_lo(b):
                dve.wait_ge(S["x2_hi"], b + 1)
                stt(x2s[:, 1], x2[:], X_UP, x2s[:, 0], ALU.mult, ALU.subtract).then_inc(S["e1b"], 1)

            def body(i, nxt, cur, prev, last):
                t8 = i * C

                def mask(t):
                    dve.wait_ge(S["ex"], t8 + t + 1)
                    s = t % RING
                    tt(att[:, s], att[:, s], adjT[:, t, :], ALU.mult).then_inc(S["pm"], 1)

                def p_lo_part(t):
                    dve.wait_ge(S["ph"], t8 + t + 1)
                    s = t % RING
                    stt(p_lo[:, s], p_hi[:, s], -LO_UP, att[:, s], ALU.mult, ALU.add).then_inc(S["pl"], 1)

                if prev:
                    l2_ch = Count(dve, S["l2_c"], i - 1, L2_LINKS)
                if cur:
                    sj_ch = Count(dve, S["sj_c"], i, 5)

                def y0_half(h):
                    split_lo(yT[:, 1, half(h)], m7[:] if is_first(i, 0) else r1[:, half(h)], Y0_DOWN, yT[:, 0, half(h)], "y0", 2 * (i + 1) + h + 1)

                def relu_residual():
                    dve.wait_ge(S["fa"], 2 * (i - 1))
                    if not is_first(i, 2):
                        dve.wait_ge(S["stored"], 16 * (i - 2))
                    stt(outb[:], u[:], 0.0, x3[:], ALU.max, ALU.add).then_inc(S["f_c"], 1)

                def finish_stats():
                    dve.wait_ge(S["f_c"], i - 1)
                    ln_stats(3, i - 2, outb)

                if last:
                    for h in range(2):
                        end_sum(i - 2, h)
                if nxt and prev and not is_first(i, 1):
                    x0_max(i + 1)
                if prev:
                    sums_read(i - 1, m7)
                if nxt and cur:
                    x0_scale_read(i + 1)
                if prev:
                    sums(i - 1)
                if cur:
                    mask(0)
                if prev:
                    l2_read(l2_ch, i - 1, m7)
                if nxt and cur:
                    x0_scales(i + 1)
                if cur:
                    for t in range(1, C):
                        mask(t)
                        p_lo_part(t - 1)
                        if prev and t == 4:
                            if last:
                                dve.wait_ge(S["f_c"], i - 1)
                            l2_rank_one(l2_ch, z_all)
                        if t == 3 and last:
                            relu_residual()
                        if t == 5 and prev:
                            y2_lo(i - 1, 0)
                        if is_first(i, 1):
                            if t in (1, 3, 6):
                                lap_row({1: 5, 3: 6, 6: 7}[t])
                            if t in (2, 5, 7):
                                lap_lo_part({2: 5, 5: 6, 7: 7}[t])
                        if is_first(i, 0):
                            if t == 1:
                                x0_lo(1)
                            if t == 3:
                                lap_lo_part(2)
                                lap_row(3)
                    if is_first(i, 0):
                        y0_half(0)
                    p_lo_part(C - 1)
                    if is_first(i, 0):
                        lap_lo_part(3)
                        lap_row(4)
                        lap_lo_part(4)
                    if nxt and prev:
                        x0_lo(i + 1)
                if is_first(i, B - 1):
                    return

                if prev:
                    y2_lo(i - 1, 1)
                if last:
                    finish_stats()
                if prev:
                    l2_row(l2_ch, z_all)
                    l2_end(l2_ch, z_all, i - 1)
                    ln_begin(2, i - 1, x3)
                if last:
                    ln_arg(3, i - 2)
                if cur:
                    row_sums(i)
                    if prev and nxt:
                        y0_half(0)
                    for j in range(C):
                        l_ = attention_residual(j)
                        if prev and j == C // 2:
                            ln_shift(2, i - 1)
                    l_.then_inc(S["e1a"], 1)
                elif prev:
                    ln_shift(2, i - 1)
                if prev:
                    ln_norm(2, i - 1, x3)
                if last:
                    ln_shift(3, i - 2)
                if nxt and not cur:
                    y0_half(0)
                if nxt:
                    c_y = small[:, 4, 2, 0:1]
                    ch = Count(dve, S["e0_c"], i + 1, 8)
                    ch.link(ts(c_y, c_y0[:], c_w0, None, ALU.mult))

                    def y_half(h):
                        hc = half_chunks(h)
                        dve.wait_ge(S["p0_mm"], 2 * (i + 1) + h + 1)
                        return stt(x1[:, hc], cd(r1[:])[:, hc], c_y, row(b0_bc[:], C // 2), ALU.mult, ALU.add)

                    if prev:
                        ch.link(y_half(0))
                        chunk_stats(4, x1, range(C // 2))
                        y0_half(1)
                    else:
                        y0_half(1)
                        ch.link(y_half(0))
                        chunk_stats(4, x1, range(C // 2))
                if prev:
                    for h in range(2):
                        x3t_lo(z_all, i - 1, h)

                if nxt:
                    ch.link(y_half(1))
                    if prev:
                        r_lo(z_all, i - 1, 0)
                        r_lo(z_all, i - 1, 1)
                    ch.link(chunk_stats(4, x1, range(C // 2, C)))
                    ch.link(tt(pair[:], stats[:, 4, :, :, 1], stats[:, 4, :, :, 1], ALU.mult))
                    ch.link(stt(pair[:], pair[:], D / 2.0, stats[:, 4, :, :, 2], ALU.mult, ALU.add))
                    ch.link(tt(small[:, 4, 0], pair[:, :, 0], pair[:, :, 1], ALU.add))
                    ch.mark(ts(small[:, 4, ARG], small[:, 4, 0], NORM_FLOOR * NORM_FLOOR, None, ALU.max))
                    ch.end()
                elif prev:
                    r_lo(z_all, i - 1, 0)
                    r_lo(z_all, i - 1, 1)
                if cur:
                    dve.wait_ge(S["e1a"], i + 1)
                    ln_stats(1, i, x2)
                if cur and not nxt:
                    ln_arg(1, i)
                if is_first(i, -1):
                    dve.wait_ge(S["dis_ok"], 1)
                    for c in range(C):
                        l_ = ts(tmp[:, c], ident[:], dis[:, c:c + 1], None, ALU.mult)
                    l_.then_inc(S["diag_ok"], 1)
                if nxt:
                    dve.wait_ge(S["norm_r"], i + 2)
                    for j in range(C):
                        l_ = stt(x1[:, j], x1[:, j], small[:, 4, ROOT, j:j + 1], x0[:, j], ALU.mult, ALU.add)
                    l_.then_inc(S["e0"], 1)
                    dve.wait_ge(S["e0"], i + 2)
                    ln_begin(0, i + 1, x1)
                if cur and nxt and not prev:
                    ln_arg(1, i)
                if prev:
                    u_part(z_all, i - 1)
                if is_first(i, -1):
                    dve.wait_ge(S["dbc_mm"], 1)
                    ts(dis_bc, r0[:], -LAP_UP / (LO_UP * P_UP), None, ALU.mult).then_inc(S["diag_ok"], 1)
                    dve.wait_ge(S["diag_ok"], 2)
                if prev:
                    q_part(z_all, i - 1, 0)
                if nxt:
                    ln_shift(0, i + 1)
                    ln_norm(0, i + 1, x1)
                if cur and not prev:
                    ln_shift(1, i)
                if is_first(i, 0):
                    x0_max(2)
                if prev:
                    ln_arg(1, i)
                    q_lo(z_all, i - 1, 0)
                if is_first(i, -1):
                    lap_row(0)

                def x1t_half(h):
                    split_lo(x1T[:, 1, half(h)], r1[:, half(h)], X_UP, x1T[:, 0, half(h)], "x1t", 2 * (i + 1) + h + 1)

                if nxt:
                    x1t_half(0)
                    x1t_half(1)
                if is_first(i, -1):
                    lap_row(1)
                if prev:
                    q_part(z_all, i - 1, 1)
                if prev:
                    ln_shift(1, i)
                    q_lo(z_all, i - 1, 1)
                if cur:
                    ln_norm(1, i, x2)
                if nxt:
                    for h in range(2):
                        split_lo(gr[:, 1, half(h)], r2[:, half(h)], W_DOWN, gr[:, 0, half(h)], "g", 2 * (i + 1) + h + 1)
                if nxt:
                    for h in range(2):
                        hc = half_chunks(h)
                        split_lo(vlo[:, hc], cd(r1[:])[:, hc], W_DOWN, vhi[:, hc, 0:D], "v", 2 * (i + 1) + h + 1)
                if is_first(i, -1):
                    x0_max(1)
                    lap_lo_part(0, 1)
                    lap_row(2)
                if cur:
                    for k_ in range(4):
                        sj_step(sj_ch, i, k_)
                    x2_lo(i)

            iterations(dve, body)
            y2_lo(B - 2, 1)
            dve.wait_ge(S["f_c"], B - 2)
            ln_stats(3, B - 3, outb)
            l2_ch = Count(dve, S["l2_c"], B - 2, L2_LINKS)
            l2_ch.n = 2
            l2_row(l2_ch, z_all)
            l2_end(l2_ch, z_all, B - 2)
            ln_begin(2, B - 2, x3)
            ln_arg(3, B - 3)
            row_sums(B - 1)
            for j in range(C):
                l_ = attention_residual(j)
                if j == C // 2:
                    ln_shift(2, B - 2)
            l_.then_inc(S["e1a"], 1)
            ln_norm(2, B - 2, x3)
            dve.wait_ge(S["e1a"], B)
            ln_begin(1, B - 1, x2)
            for h in range(2):
                x3t_lo(z_all, B - 2, h)
            ln_shift(3, B - 3)
            ln_shift(1, B - 1)
            ln_norm(1, B - 1, x2)
            x2_lo(B - 1)
            for h in range(2):
                r_lo(z_all, B - 2, h)
            sj_ch = Count(dve, S["sj_c"], B - 1, 5)
            for k_ in range(3):
                sj_step(sj_ch, B - 1, k_)
            y2_lo(B - 1, 0)
            sj_step(sj_ch, B - 1, 3)
            u_part(z_all, B - 2)
            sums_read(B - 1, av[:, 2])
            sums(B - 1)
            l2_ch = Count(dve, S["l2_c"], B - 1, L2_LINKS)
            l2_read(l2_ch, B - 1, av[:, 2])
            dve.wait_ge(S["pl"], C * B)
            l2_rank_one(l2_ch, z_end)
            y2_lo(B - 1, 1)
            l2_row(l2_ch, z_end)
            l2_end(l2_ch, z_end, B - 1)
            ln_begin(2, B - 1, z_end.x3)
            q_part(z_all, B - 2, 0)
            ln_shift(2, B - 1)
            ln_norm(2, B - 1, z_end.x3)
            q_part(z_all, B - 2, 1)
            q_lo(z_all, B - 2, 0)
            for h in range(2):
                x3t_lo(z_end, B - 1, h)
            q_lo(z_all, B - 2, 1)
            for h in range(2):
                r_lo(z_end, B - 1, h)
            u_part(z_end, B - 1)
            for h in range(2):
                q_part(z_end, B - 1, h)
            for h in range(2):
                q_lo(z_end, B - 1, h)
            for h in range(2):
                end_sum(B - 2, h)
            dve.wait_ge(S["fa"], 2 * (B - 1))
            dve.wait_ge(S["stored"], 16 * (B - 2))
            stt(outb[:], u[:], 0.0, x3[:], ALU.max, ALU.add).then_inc(S["f_c"], 1)
            dve.wait_ge(S["f_c"], B - 1)
            ln_begin(3, B - 2, outb)
            ln_shift(3, B - 2)
            z = z_end

            def end_part(h, first, end):
                hc = slice(first, end)
                dve.wait_ge(S["o_mm"], 2 * B - 1 + h)
                stt(z.u[:, hc], cd((r1[:], r2)[h])[:, hc], c_o, z.u[:, hc], ALU.mult, ALU.add).then_inc(S["fa"], 1)
                dve.wait_ge(S["fa"], 2 * B - 1 + h)
                stt(z.outb[:, hc], z.u[:, hc], 0.0, z.x3[:, hc], ALU.max, ALU.add).then_inc(S["f_c"], 1)
                dve.wait_ge(S["f_c"], B + h)
                chunk_stats(END, z.outb, range(first, end)).then_inc(S["ln3"], 1)
                ln_arg(3, B - 1, hc, END, LN_ARG * h)

            def end_norm(h, first, end):
                dve.wait_ge(S["ln3_r"], B + h)
                sm = small[:, END, :, first:end]
                links = LN_LINKS * (B - 1) + 2 * LN_ARG + 1 + h
                tt(sm[:, SHIFT], sm[:, 4], sm[:, ROOT], ALU.mult).then_inc(S["ln3"], 1)
                dve.wait_ge(S["ln3"], links)
                for j in range(first, (first + end) // 2):
                    l_ = ts(z.outb[:, j], z.outb[:, j], small[:, END, ROOT, j:j + 1], small[:, END, SHIFT, j:j + 1],
                            ALU.mult, ALU.add)
                l_.then_inc(S["ln3_v"], 1)

            for h, part in enumerate(END_PARTS):
                end_part(h, *part)
            for h, part in enumerate(END_PARTS):
                end_norm(h, *part)

        @block.tensor
        def _(pe):
            mm = nc.tensor.matmul

            pe.wait_ge(S["x_max"], 1)
            pe.wait_ge(S["const_ok"], 1)
            mm(m7[:, 4:5], ones[:], xmax[:], start=True, stop=True).then_inc(S["x_sum"], 1)
            pe.wait_ge(S["ident_ok"], 3)
            pe.wait_ge(S["wq_in"], 32)
            pe.wait_ge(S["x_st"], 1)
            nc.tensor.transpose(m7[:, 0:P], q_sb, ident[:])
            nc.tensor.transpose(m7[:, P:2 * P], k_sb, ident[:]).then_inc(S["qk_t"], 1)

            def split_product(dst, s_hi, s_lo, m_hi, m_lo, start, stop):
                mm(dst, s_hi, m_hi, start=start, stop=False, skip_group_check=True)
                mm(dst, s_hi, m_lo, start=False, stop=False, skip_group_check=True)
                return mm(dst, s_lo, m_hi, start=False, stop=stop, skip_group_check=True)

            def transpose_half(dst, src, h):
                for j in range(h * C // 2, (h + 1) * C // 2):
                    l_ = nc.tensor.transpose(dst[:, chunk(j)], src[:, j], ident[:])
                return l_

            def project_half(dst, srcT, w_hi, w_lo, h):
                for j in range(h * C // 2, (h + 1) * C // 2):
                    l_ = split_product(dst[:, chunk(j)], srcT[:, 0, chunk(j)], srcT[:, 1, chunk(j)], w_hi, w_lo, True, True)
                return l_

            def project(dst, srcT, w_hi, w_lo):
                project_half(dst, srcT, w_hi, w_lo, 0)
                return project_half(dst, srcT, w_hi, w_lo, 1)

            def apply_laplacian(dst, src, first, last_):
                for j in range(first, last_):
                    for m in range(C):
                        l_ = split_product(dst[:, chunk(j)], lap[:, 0, m, chunk(j)], lap[:, 1, m, chunk(j)],
                                           src[:, 0, chunk(m)], src[:, 1, chunk(m)], m == 0, m == C - 1)
                return l_

            def adj_x0(h, first=0, last_=C, dst=r1, at=None):
                own = [m for m in range(C) if m // (C // 2) == h]
                order = own + [m for m in range(C) if m not in own]
                for n_ in range(first, last_):
                    m = order[n_]
                    l_ = split_product(dst[:, half(h if at is None else at)], x0s[:, 0, m], x0s[:, 1, m], a_hi[:, m, half(h)],
                                       a_lo[:, m, half(h)], n_ == 0, n_ == C - 1)
                    if m in own:
                        for part in range(2):
                            mm(dst[:, chunk(m if at is None else m % (C // 2))], x0s[:, part, m], ident_up[:], start=False, stop=False,
                               skip_group_check=True)
                if last_ == C:
                    l_.then_inc(S["y0_mm"], 1)

            def adj_x2_part(b, part):
                h, m0 = part // 4, 2 * (part % 4)
                if part == 4:
                    pe.wait_ge(S["y2_lo"], 2 * b + 1)
                for m in range(m0, m0 + 2):
                    l_ = split_product(m7[:], x2s[:, 0, m], x2s[:, 1, m], a_hi[:, m, half(h)], a_lo[:, m, half(h)],
                                       m == 0, m == C - 1)
                if part % 4 == 3:
                    l_.then_inc(S["y2_mm"], 1)

            def sum_x2(dst):
                for j in range(C):
                    mm(dst[:, 0:3], x2s[:, 0, j], one_sj[:, j], start=(j == 0), stop=False, skip_group_check=True)
                    l_ = mm(dst[:, 0:2], x2s[:, 1, j], one_sj[:, j, 0:2], start=False, stop=(j == C - 1),
                            skip_group_check=True)
                l_.then_inc(S["xx_mm"], 1)

            def sums_w2(dst, b):
                pe.wait_ge(S["xb_ok"], b + 1)
                mm(dst[:, 0:P], xb[:, 0], w2_sb[:], start=True, stop=True)
                mm(dst[:, P:2 * P], xb[:, 1], w2_sb[:], start=True, stop=True).then_inc(S["rr_mm"], 1)

            for c in range(C):
                pe.wait_ge(adj_in[c], 16)
                if c >= 2:
                    pe.wait_ge(S["adj_cp"], c - 1)
                buf = (r0[:], r2)[c % 2]
                for m in range(C):
                    l_ = nc.tensor.transpose(buf[:, chunk(m)], adj_rows[:, c, chunk(m)], ident[:])
                l_.then_inc(S["tr"], 1)
                if c == 0:
                    pe.wait_ge(S["qk_c"], 1)
                    mm(m7[:, 2 * P:3 * P], qT, kT, start=True, stop=True).then_inc(S["m_mm"], 1)
                if c == C - 1:
                    pe.wait_ge(S["m_cp"], 1)
                    pe.wait_ge(S["w_max"], 5)
                    mm(m7[:, 3 * P:3 * P + 5], ones[:], wmax[:], start=True, stop=True).then_inc(S["w_sum"], 1)
                if c >= C - 3:
                    if c == C - 3:
                        pe.wait_ge(S["x_lo"], 1)
                        pe.wait_ge(S["adj_lo"], 1 + C // 2)
                    adj_x0(0, 2 * (c - C + 3), 2 * (c - C + 4))
            adj_x0(0, C - 2)
            pe.wait_ge(S["adj_lo"], C + 1)

            def body(i, nxt, cur, prev, last):
                t8 = i * C

                def scores(t):
                    if t == 0:
                        pe.wait_ge(S["v_lo"], 2 * (i + 1))
                    elif t == 1:
                        if last:
                            pe.wait_ge(S["fa"], 2 * (i - 1))
                    else:
                        pe.wait_ge(S["th"], t8 + t - 1)
                    dst = (r1, r0)[t % 2]
                    for h in range(2):
                        l_ = split_product(dst[:, half(h)], x1T[:, 0, chunk(t)], x1T[:, 1, chunk(t)],
                                           gr[:, 0, half(h)], gr[:, 1, half(h)], True, True)
                    l_.then_inc(S["s_mm"], 1)

                def attend(t):
                    pe.wait_ge(S["pl"], t8 + t + 1)
                    if t == 0 and not is_first(i, 0):
                        pe.wait_ge(S["e1a"], i)
                    s = t % RING
                    for j in range(C):
                        o = (j % 3) * AVW
                        acc = av[:, j // 3, o:o + D + 1]
                        mm(acc, p_hi[:, s, chunk(j)], vhi[:, t, 0:D + 1], start=(t == 0 and j % 3 == 0), stop=False,
                           skip_group_check=True)
                        mm(acc[:, 0:D], p_hi[:, s, chunk(j)], vlo[:, t, :], start=False, stop=False, skip_group_check=True)
                        l_ = mm(acc, p_lo[:, s, chunk(j)], vhs[:, t, 0:D + 1], start=False, stop=(t == C - 1),
                                skip_group_check=True)
                    l_.then_inc(S["av_mm"], 1)

                def adj_x2(part):
                    if part == 0:
                        pe.wait_ge(S["l2_c"], L2_LINKS * (i - 1) + 1)
                    adj_x2_part(i - 1, part)

                def sums():
                    pe.wait_ge(S["e1b"], i)
                    if last:
                        pe.wait_ge(S["y2_lo"], 2 * (i - 1))
                    sum_x2(m7)

                def y0_early(h, n_):
                    if n_ == 0 and h == 0:
                        pe.wait_ge(S["x_lo"], 2)
                    if n_ == 0 and h == 1:
                        pe.wait_ge(S["y0_lo"], 3)
                    adj_x0(h, n_, n_ + 2, m7, 0)

                late = is_first(i, 0) or is_first(i, 1)
                if cur:
                    scores(0)
                    scores(1)
                if late:
                    scores(2)
                if is_first(i, 1):
                    scores(3)
                if nxt and cur:
                    if last:
                        pe.wait_ge(S["y2_lo"], 2 * (i - 1))
                    pe.wait_ge(S["x_max"], i + 2)
                    mm(m7[:, 4:5], ones[:], xmax[:], start=True, stop=True).then_inc(S["x_sum"], 1)
                if prev:
                    sums()
                if cur and not late:
                    scores(2)
                if prev:
                    if nxt:
                        pe.wait_ge(S["x_st"], 5 * (i + 1) + 1)
                    sums_w2(m7, i - 1)
                for t in range(AHEAD, C):
                    if cur and not (is_first(i, 1) and t == 3):
                        scores(t)
                    if prev and t == AHEAD:
                        adj_x2(0)
                        adj_x2(1)
                    if cur:
                        attend(t - AHEAD)
                    if prev and AHEAD < t < C - 2:
                        adj_x2(t - AHEAD + 1)
                    if is_first(i, 0) and t > AHEAD:
                        y0_early(0, 2 * (t - AHEAD - 1))
                if prev:
                    adj_x2(C - AHEAD - 1)
                for t in range(C - AHEAD, C):
                    if cur:
                        attend(t)
                    if prev and t == C - AHEAD:
                        for part in range(t, C):
                            adj_x2(part)
                    if is_first(i, 0):
                        if t == C - 2:
                            y0_early(1, 0)
                            y0_early(1, 2)
                        if t == C - 1:
                            y0_early(1, 4)
                            y0_early(1, 6)
                if is_first(i, B - 1):
                    return
                if prev:
                    pe.wait_ge(S["y2_lo"], 2 * i)
                    if cur:
                        pe.wait_ge(S["th"], t8 + C)
                    project(r0, yT, w2s[:, 0], w2s[:, 1]).then_inc(S["p2_mm"], 1)
                if nxt:
                    if cur:
                        pe.wait_ge(S["th"], t8 + C - 1)
                    if prev:
                        pe.wait_ge(S["x_lo"], i + 2)
                        adj_x0(0)
                    if prev or not cur:
                        adj_x0(1, 0, C - 3)

                def layer0_half(h):
                    pe.wait_ge(S["y0_lo"], 2 * (i + 1) + h + 1)
                    project_half(r1, yT, w0s[:, 0], w0s[:, 1], h).then_inc(S["p0_mm"], 1)

                if nxt:
                    if is_first(i, -1):
                        adj_x0(1, C - 3)
                        pe.wait_ge(S["w_red"], 12)
                    layer0_half(0)
                    if prev:
                        adj_x0(1, C - 3)
                if prev:
                    pe.wait_ge(S["ln2_v"], i)
                    transpose_half(r0, x3, 0).then_inc(S["x3t_mm"], 1)
                    pe.wait_ge(S["ln2_a"], i)
                    transpose_half(r0, x3, 1).then_inc(S["x3t_mm"], 1)
                if nxt:
                    layer0_half(1)
                if prev:
                    if cur:
                        pe.wait_ge(S["e1a"], i + 1)
                    for h in range(2):
                        pe.wait_ge(S["x3t_lo"], 2 * (i - 1) + h + 1)
                        project_half(r2, xq, w3s[:, 0, 0], w3s[:, 0, 1], h).then_inc(S["r_mm"], 1)
                    project(r0, xq, w3s[:, 1, 0], w3s[:, 1, 1]).then_inc(S["p_mm"], 1)
                    pe.wait_ge(S["r_lo"], 2 * i - 1)
                    project_half(r2, xq, w3s[:, 2, 0], w3s[:, 2, 1], 0)
                    pe.wait_ge(S["r_lo"], 2 * i)
                    project_half(r2, xq, w3s[:, 2, 0], w3s[:, 2, 1], 1).then_inc(S["u_mm"], 1)
                    pe.wait_ge(S["p_cp"], i)
                    if is_first(i, 1):
                        pe.wait_ge(S["lap_lo"], C)
                    apply_laplacian(r0, gr, 0, C // 2).then_inc(S["t_mm"], 1)
                    apply_laplacian(r0, gr, C // 2, C - 1)
                if is_first(i, -1):
                    pe.wait_ge(S["diag_ok"], 1)
                    for c in range(C):
                        l_ = mm(r0[:, chunk(c)], ones[:], tmp[:, c], start=True, stop=True)
                    l_.then_inc(S["dbc_mm"], 1)
                if nxt:
                    pe.wait_ge(S["ln0_v"], i + 2)
                    transpose_half(r1, x1, 0).then_inc(S["x1t_mm"], 1)
                    pe.wait_ge(S["ln0_a"], i + 2)
                    transpose_half(r1, x1, 1).then_inc(S["x1t_mm"], 1)
                if prev:
                    apply_laplacian(r0, gr, C - 1, C).then_inc(S["t_mm"], 1)
                if nxt:
                    if prev:
                        pe.wait_ge(S["u_ok"], i)
                    for h in range(2):
                        pe.wait_ge(S["x1t_lo"], 2 * (i + 1) + h + 1)
                        split_product(r2[:, half(h)], ms[:, 0], ms[:, 1], x1T[:, 0, half(h)], x1T[:, 1, half(h)],
                                      True, True).then_inc(S["g_mm"], 1)
                    for h in range(2):
                        project_half(r1, x1T, vs[:, 0], vs[:, 1], h).then_inc(S["v_mm"], 1)
                if prev:
                    pe.wait_ge(S["q_lo"], 2 * i)
                    for h in range(2):
                        apply_laplacian(r0, xq, h * C // 2, (h + 1) * C // 2).then_inc(S["o_mm"], 1)

            def x3_t(z, b):
                pe.wait_ge(S["ln2_v"], b + 1)
                transpose_half(z.acc, z.x3, 0).then_inc(S["x3t_mm"], 1)
                pe.wait_ge(S["ln2_a"], b + 1)
                transpose_half(z.acc, z.x3, 1).then_inc(S["x3t_mm"], 1)

            def r_product(z, b):
                for h in range(2):
                    pe.wait_ge(S["x3t_lo"], 2 * b + h + 1)
                    project_half(r2, z.xq, w3s[:, 0, 0], w3s[:, 0, 1], h).then_inc(S["r_mm"], 1)

            def p_product(z):
                project(z.acc, z.xq, w3s[:, 1, 0], w3s[:, 1, 1]).then_inc(S["p_mm"], 1)

            def u_product(z, b):
                pe.wait_ge(S["r_lo"], 2 * b + 1)
                project_half(r2, z.xq, w3s[:, 2, 0], w3s[:, 2, 1], 0)
                pe.wait_ge(S["r_lo"], 2 * b + 2)
                project_half(r2, z.xq, w3s[:, 2, 0], w3s[:, 2, 1], 1).then_inc(S["u_mm"], 1)

            iterations(pe, body)
            pe.wait_ge(S["y2_lo"], 2 * (B - 1))
            pe.wait_ge(S["th"], C * B)
            project(r0, yT, w2s[:, 0], w2s[:, 1]).then_inc(S["p2_mm"], 1)
            x3_t(z_all, B - 2)
            pe.wait_ge(S["e1a"], B)
            r_product(z_all, B - 2)
            p_product(z_all)
            pe.wait_ge(S["e1b"], B)
            for part in range(4):
                adj_x2_part(B - 1, part)
            u_product(z_all, B - 2)
            pe.wait_ge(S["p_cp"], B - 1)
            apply_laplacian(r0, gr, 0, 1)
            pe.wait_ge(S["sj_c"], 5 * B)
            sum_x2(av[:, 2])
            adj_x2_part(B - 1, 4)
            sums_w2(av[:, 2], B - 1)
            for part in range(5, 8):
                adj_x2_part(B - 1, part)
            apply_laplacian(r0, gr, 1, 3)
            pe.wait_ge(S["y2_lo"], 2 * B)
            project(r1, yT, w2s[:, 0], w2s[:, 1]).then_inc(S["p2_mm"], 1)
            apply_laplacian(r0, gr, 3, C // 2).then_inc(S["t_mm"], 1)
            apply_laplacian(r0, gr, C // 2, C).then_inc(S["t_mm"], 1)
            x3_t(z_end, B - 1)
            pe.wait_ge(S["u_ok"], B - 1)
            r_product(z_end, B - 1)
            p_product(z_end)
            u_product(z_end, B - 1)
            pe.wait_ge(S["p_cp"], B)
            for h in range(2):
                apply_laplacian(r1, z_end.gr, h * C // 2, (h + 1) * C // 2).then_inc(S["t_mm"], 1)
            pe.wait_ge(S["q_lo"], 2 * (B - 1))
            for h in range(2):
                apply_laplacian(r0, xq, h * C // 2, (h + 1) * C // 2).then_inc(S["o_mm"], 1)
            pe.wait_ge(S["q_lo"], 2 * B)
            for h, (first, end) in enumerate(END_PARTS):
                if h == 1:
                    pe.wait_ge(S["u_ok"], B)
                apply_laplacian((r1, r2)[h], z_end.xq, first, end).then_inc(S["o_mm"], 1)


_INS = ["x", "adj", "L0_gnn_weight", "L0_gnn_bias", "L1_gnn_q", "L1_gnn_k", "L1_gnn_v", "L2_gnn_g_w", "L2_gnn_g_b",
        "L2_gnn_weight", "L2_gnn_bias", "L3_gnn_weight", "L3_gnn_bias"]


def kernel(**inputs):
    import numpy as _np
    import concourse.bacc as _bacc
    from concourse import mybir as _mybir
    from concourse.bass_utils import run_bass_kernel_spmd as _run

    nc = _bacc.Bacc("TRN2", target_bir_lowering=False, num_devices=1)
    arrays, args = {}, []
    for name in _INS:
        a = _np.ascontiguousarray(inputs[name])
        if a.ndim == 0:
            a = a.reshape(1)
        arrays[f"in_{name}"] = a
        args.append(nc.dram_tensor(f"in_{name}", a.shape, _mybir.dt.from_np(a.dtype), kind="ExternalInput").ap())
    args.append(nc.dram_tensor("out_0", (B, N, D), _mybir.dt.float32, kind="ExternalOutput").ap())
    adj_resnorm(nc, *args)
    r = _run(nc, [arrays], core_ids=[0])
    return r.results[0]["out_0"]
```
